# Optimizing a Trainium2 kernel written in Bass

```python
import numpy as np
import jax
import jax.numpy as jnp

def _softmax(x, axis=-1):
    return jax.nn.softmax(x, axis=axis)

def _gelu(x):
    return jax.nn.gelu(x, approximate=True)

def _silu(x):
    return jax.nn.silu(x)

def _sigmoid(x):
    return jax.nn.sigmoid(x)

def _layernorm(x, axis=-1, eps=1e-05):
    m = jnp.mean(x, axis=axis, keepdims=True)
    v = jnp.var(x, axis=axis, keepdims=True)
    return (x - m) / jnp.sqrt(v + eps)

def _scatter_add(tgt, idx, src, axis=0):
    return tgt.at[idx].add(src)

def _segment_sum(src, seg, n):
    return jax.ops.segment_sum(src, seg, n)
kernel_name = 'mk_sandwich_d1_jaxref_r4_263028'

def setup_inputs(seed: int=0):
    np.random.seed(seed)
    _w = jnp.asarray

    def _L0_attn_setup():
        import jax, jax.numpy as jnp
        import numpy as np
        B, S, DM = (2, 512, 512)
        H, KVH, HD = (16, 4, 128)
        REP = H // KVH
        ROPE_BASE = 10000.0
        EPS = 1e-06

        def _rope_tables(seq_len, dim):
            inv_freq = 1.0 / ROPE_BASE ** (jnp.arange(0, dim, 2, dtype=jnp.float32) / dim)
            t = jnp.arange(seq_len, dtype=jnp.float32)
            freqs = jnp.outer(t, inv_freq)
            emb = jnp.concatenate([freqs, freqs], -1)
            return (jnp.cos(emb), jnp.sin(emb))

        def _rotate_half(x):
            d = x.shape[-1] // 2
            return jnp.concatenate([-x[..., d:], x[..., :d]], axis=-1)
        key = jax.random.key(seed)
        k0, k1, k2, k3, k4 = jax.random.split(key, 5)
        w = lambda k, o, i: jax.random.normal(k, (o, i), jnp.float32) * (1.0 / np.sqrt(i))
        return {'x': jax.random.normal(k0, (B, S, DM), jnp.float32), 'Wq': w(k1, H * HD, DM), 'Wk': w(k2, KVH * HD, DM), 'Wv': w(k3, KVH * HD, DM), 'Wo': w(k4, DM, H * HD)}
    _L0_attn_in = _L0_attn_setup()

    def _L0_ffn_setup():
        import jax, jax.numpy as jnp
        import numpy as np

        def _sparsify_2to4(h):
            B, S, I = h.shape
            g = h.reshape(B, S, I // 4, 4)
            a = jnp.abs(g)
            _, idx = jax.lax.top_k(a, 2)
            pos = jnp.arange(4)
            mask = (pos == idx[..., 0:1]) | (pos == idx[..., 1:2])
            return (g * mask.astype(g.dtype)).reshape(B, S, I)
        key = jax.random.key(seed)
        k1, k2, k3, k4 = jax.random.split(key, 4)
        B, S, H, I = (4, 512, 512, 2048)
        x = jax.random.normal(k1, (B, S, H), dtype=jnp.float32)
        w_gate = jax.random.normal(k2, (H, I), dtype=jnp.float32) / np.sqrt(H)
        w_up = jax.random.normal(k3, (H, I), dtype=jnp.float32) / np.sqrt(H)
        w_down = jax.random.normal(k4, (I, H), dtype=jnp.float32) / np.sqrt(I)
        return {'x': x, 'w_gate': w_gate, 'w_up': w_up, 'w_down': w_down}
    _L0_ffn_in = _L0_ffn_setup()
    _d = {'L0_attn_x': _L0_attn_in['x'], 'L0_attn_Wq': _L0_attn_in['Wq'], 'L0_attn_Wk': _L0_attn_in['Wk'], 'L0_attn_Wv': _L0_attn_in['Wv'], 'L0_attn_Wo': _L0_attn_in['Wo'], 'L0_ffn_w_gate': _L0_ffn_in['w_gate'], 'L0_ffn_w_up': _L0_ffn_in['w_up'], 'L0_ffn_w_down': _L0_ffn_in['w_down']}
    _x0 = _d['L0_attn_x']
    _d['L0_attn_x'] = jax.random.normal(jax.random.fold_in(jax.random.key(seed), 1), (2, 1024, 512), dtype=_x0.dtype)
    del _x0
    return _d

def reference(L0_attn_x, L0_attn_Wq, L0_attn_Wk, L0_attn_Wv, L0_attn_Wo, L0_ffn_w_gate, L0_ffn_w_up, L0_ffn_w_down):

    def _L0_attn_ref(x, Wq, Wk, Wv, Wo):
        import jax, jax.numpy as jnp
        import numpy as np
        B, S, DM = (2, 512, 512)
        H, KVH, HD = (16, 4, 128)
        REP = H // KVH
        ROPE_BASE = 10000.0
        EPS = 1e-06

        def _rope_tables(seq_len, dim):
            inv_freq = 1.0 / ROPE_BASE ** (jnp.arange(0, dim, 2, dtype=jnp.float32) / dim)
            t = jnp.arange(seq_len, dtype=jnp.float32)
            freqs = jnp.outer(t, inv_freq)
            emb = jnp.concatenate([freqs, freqs], -1)
            return (jnp.cos(emb), jnp.sin(emb))

        def _rotate_half(x):
            d = x.shape[-1] // 2
            return jnp.concatenate([-x[..., d:], x[..., :d]], axis=-1)
        bsz, seq_len, _ = x.shape
        q = (x @ Wq.T).reshape(bsz, seq_len, H, HD).transpose(0, 2, 1, 3)
        k = (x @ Wk.T).reshape(bsz, seq_len, KVH, HD).transpose(0, 2, 1, 3)
        v = (x @ Wv.T).reshape(bsz, seq_len, KVH, HD).transpose(0, 2, 1, 3)
        cos, sin = _rope_tables(seq_len, HD)
        cos, sin = (cos[None, None], sin[None, None])
        q = q * cos + _rotate_half(q) * sin
        k = k * cos + _rotate_half(k) * sin
        k = jnp.repeat(k, REP, axis=1)
        v = jnp.repeat(v, REP, axis=1)
        qf = jax.nn.elu(q) + 1.0
        kf = jax.nn.elu(k) + 1.0
        qf_t = qf.transpose(2, 0, 1, 3)
        kf_t = kf.transpose(2, 0, 1, 3)
        v_t = v.transpose(2, 0, 1, 3)

        def step(carry, inp):
            state, z = carry
            q_s, k_s, v_s = inp
            state = state + k_s[..., :, None] * v_s[..., None, :]
            z = z + k_s
            num = jnp.einsum('bhe,bhed->bhd', q_s, state)
            den = jnp.einsum('bhe,bhe->bh', q_s, z)[..., None] + EPS
            return ((state, z), num / den)
        init = (jnp.zeros((bsz, H, HD, HD), x.dtype), jnp.zeros((bsz, H, HD), x.dtype))
        _, out = jax.lax.scan(step, init, (qf_t, kf_t, v_t))
        out = out.transpose(1, 0, 2, 3).reshape(bsz, seq_len, H * HD)
        return out @ Wo.T

    def _L0_ffn_ref(x, w_gate, w_up, w_down):
        import jax, jax.numpy as jnp
        import numpy as np

        def _sparsify_2to4(h):
            B, S, I = h.shape
            g = h.reshape(B, S, I // 4, 4)
            a = jnp.abs(g)
            _, idx = jax.lax.top_k(a, 2)
            pos = jnp.arange(4)
            mask = (pos == idx[..., 0:1]) | (pos == idx[..., 1:2])
            return (g * mask.astype(g.dtype)).reshape(B, S, I)
        h = jax.nn.silu(jnp.einsum('bsh,hi->bsi', x, w_gate)) * jnp.einsum('bsh,hi->bsi', x, w_up)
        h_sparse = _sparsify_2to4(h)
        return jnp.einsum('bsi,ih->bsh', h_sparse, w_down)
    x = L0_attn_x
    x = x + _layernorm(_L0_attn_ref(_layernorm(x, axis=-1), L0_attn_Wq, L0_attn_Wk, L0_attn_Wv, L0_attn_Wo), axis=-1)
    x = x + _layernorm(_L0_ffn_ref(_layernorm(x, axis=-1), L0_ffn_w_gate, L0_ffn_w_up, L0_ffn_w_down), axis=-1)
    return x

_drawn_inputs = setup_inputs


def setup_inputs(seed=0):
    import zlib

    import numpy as np

    out = dict(_drawn_inputs(seed))
    spreads = {}
    factors = {}
    for name, (base, spread) in spreads.items():
        noise = np.random.default_rng([zlib.crc32(name.encode()), seed]).standard_normal(out[name].shape)
        drawn = base * np.exp(spread * noise) if base else spread * noise
        out[name] = jnp.asarray(drawn.astype(out[name].dtype))
    for name, factor in factors.items():
        out[name] = (out[name] * factor).astype(out[name].dtype)
    return out
```

```python
from contextlib import ExitStack

import numpy as np

import concourse.bass as bass
from concourse import mybir

ALU = mybir.AluOpType
ACT = mybir.ActivationFunctionType
F32 = mybir.dt.float32
F32R = mybir.dt.float32r
BF16 = mybir.dt.bfloat16

P = 128
B, S, DM = 2, 1024, 512
KVH, REP = 4, 4
W = 512
KT = DM // P
TT = S // P
HALF = P // 2
NU = 4
SPU = 8
EPS_LN = 1e-5
EPS_DEN = 1e-6
VP = P + 2

RING_A, RING_F = 5, 4
A_PRO, A_UNIT = 6, 10
F_PRO, F_UNIT = 8, 12

T_SLOT = NU * SPU
T_ITEM = 5 * 2 * NU
T_KV = 2 * 2 * NU
T_STEP = 2 * NU
T_STATE = 7 * NU
T_WPOOL_A = A_PRO + 9 * (NU - 1) + 4
T_WQ0 = NU - 1
T_WACT_A = A_PRO + 10 * (NU - 1) + 4
T_W_F = F_PRO + F_UNIT * (NU - 1) + 4


def item_of(m):
    return m + 5 + max(0, (m + 1) // 4 + (1 if m >= -1 else 0))


def key_item_of(m):
    return item_of(m) + 1


def build(nc, x, wq, wk, wv, wo, wg, wu, wd, cos_t, sin_t, causal, eye, out):
    with ExitStack() as ctx:
        def sb(name, shape, dtype=F32):
            return ctx.enter_context(nc.sbuf_tensor(name, shape, dtype))

        def sem(name):
            return ctx.enter_context(nc.semaphore(name))

        Xh = sb("x_hi", [P, KT, S], F32R)
        Xl = sb("x_lo", [P, KT, S], F32R)
        Y = sb("y_acc", [P, TT, DM])
        Wh = sb("w_hi", [P, 8, W], F32R)
        Wl = sb("w_lo", [P, 8, W], F32R)
        Oh = sb("wout_hi", [P, 4, W], F32R)
        Ol = sb("wout_lo", [P, 4, W], F32R)
        stage = sb("stage", [P, RING_A, W])
        big_h = sb("big_hi", [P, 2, 4, W], F32R)
        big_l = sb("big_lo", [P, 2, 4, W], F32R)
        Kh = sb("k_hi", [P, W], F32R)
        Kl = sb("k_lo", [P, W], F32R)
        KTh = sb("kt_hi", [P, 4, P], F32R)
        KTl = sb("kt_lo", [P, 4, P], F32R)
        Vh = sb("v_hi", [P, 4, VP], F32R)
        Vl = sb("v_lo", [P, 4, P], F32R)
        Sh = sb("s_hi", [P, 4, P], F32R)
        Sl = sb("s_lo", [P, 4, P], F32R)
        Ah = sb("a_hi", [P, 4, P], F32R)
        Al = sb("a_lo", [P, 4, P], F32R)
        Sth = sb("st_hi", [P, 2, P], F32R)
        Stl = sb("st_lo", [P, 2, P], F32R)
        ones = sb("ones", [P, P], F32R)
        mask = sb("mask", [P, P])
        ident = sb("ident", [P, P])
        scr = sb("scratch", [P, 19, W])
        msk = sb("masks", [P, 7, W], BF16)
        stat = sb("stat", [P, 2, 6])
        mv = sb("mv", [P, 2, 2])
        rstd = sb("rstd", [P, 2])
        mhalf = sb("mhalf", [P, 2])
        eps_den = sb("eps_den", [P, 1])
        eps_ln = sb("eps_ln", [P, 2])

        rot, xq, Eq, fq, vT, xk, Ek, kf, Sf, r0, Tn, of = [scr[:, i, :] for i in range(12)]
        cosb = scr[:, 12:14, :]
        sinb = scr[:, 14:16, :]
        YF = scr[:, 0:8, :]
        hid = scr[:, 8:12, :]
        ab = scr[:, 12:16, :]
        sg = scr[:, 16, :]
        Wmax = scr[:, 17:19, :]
        c01, c23, pw, qw, rr, m0, m2 = [msk[:, i, :] for i in range(7)]
        xt = scr[:, 16:18, :]
        xn = [scr[:, 18, :], scr[:, 11, :]]
        yt = scr[:, 9:11, :]

        bank = [ctx.enter_context(nc.psum_tensor(f"bank{i}", [P, W], F32)) for i in range(8)]
        psS, psQ, psK, psO, psD, psY, psSt, psT = bank
        psG, psU, psYF = bank[0:2], bank[2:4], bank[4:6]
        psX = bank[6:8]

        const_ld = sem("const_ld")
        const_ok = sem("const_ok")
        tab_ld = sem("tab_ld")
        ld_a = [sem(f"ld_a{i}") for i in range(RING_A)]
        ld_f = [sem(f"ld_f{i}") for i in range(RING_F)]
        act_w = sem("act_w")
        pool_w = sem("pool_w")
        dve_wq0 = sem("dve_wq0")
        act_wf = sem("act_wf")
        pool_wf = sem("pool_wf")
        ld_x = [sem("ld_x0"), sem("ld_x1")]
        st_out = [sem("st_out0"), sem("st_out1")]
        ln_var = sem("ln_var")
        pool_rs = sem("pool_rs")
        dve_xn = sem("dve_xn")
        pe_xt = sem("pe_xt")
        act_xh = sem("act_xh")
        dve_xl = sem("dve_xl")
        dve_res = sem("dve_res")
        dve_out = sem("dve_out")
        dve_self = sem("dve_self")
        dve_const = sem("dve_const")
        pool_eps = sem("pool_eps")
        passed = sem("passed")
        pe_q = sem("pe_q")
        pe_kv = sem("pe_kv")
        pe_tr = sem("pe_tr")
        pe_s = sem("pe_s")
        pe_pv = sem("pe_pv")
        pe_st = sem("pe_st")
        pe_y = sem("pe_y")
        act_rot = sem("act_rot")
        act_exp = sem("act_exp")
        act_fh = sem("act_fh")
        act_vt = sem("act_vt")
        act_kvh = sem("act_kvh")
        act_ln = sem("act_ln")
        act_r0 = sem("act_r0")
        act_sh = sem("act_sh")
        act_sth = sem("act_sth")
        act_ah = sem("act_ah")
        dve_t1 = sem("dve_t1")
        dve_t2 = sem("dve_t2")
        dve_x = sem("dve_x")
        dve_m = sem("dve_m")
        dve_f = sem("dve_f")
        dve_sf = sem("dve_sf")
        dve_T = sem("dve_T")
        dve_U = sem("dve_U")
        dve_a = sem("dve_a")
        dve_kvl = sem("dve_kvl")
        dve_stl = sem("dve_stl")
        dve_y = sem("dve_y")
        pool_fl = sem("pool_fl")
        pool_sl = sem("pool_sl")
        pool_al = sem("pool_al")
        pe_g = sem("pe_g")
        pe_u = sem("pe_u")
        pe_d = sem("pe_d")
        act_sg = sem("act_sg")
        act_ab = sem("act_ab")
        act_hh = sem("act_hh")
        dve_h = sem("dve_h")
        dve_rank = sem("dve_rank")
        dve_hs = sem("dve_hs")
        dve_hl = sem("dve_hl")
        dve_yf = sem("dve_yf")
        pool_hl = sem("pool_hl")

        block = ctx.enter_context(nc.Block())

        def need(eng, s, b, total, U, per_unit, k):
            if isinstance(U, int):
                k, U = k + U * per_unit, None
                if k <= 0:
                    return
                eng.wait_ge(s, b * total + k)
            else:
                assert k > 0
                eng.wait_ge(s, b * total + U * per_unit + k)

        def wait_apart(eng, s, value):
            eng.wait_ge(s, value)
            eng.sem_inc(passed, 1)

        pieces_a = [[0, 1], [2], [3], [4, 5]]
        pieces_f = [[0, 1], [2, 3], [4, 5], [6, 7]]
        first_unit = [[0, 1, 2, 3, 4, 5], [0, 4, 1, 5, 2, 6, 3, 7]]

        def walk_a(eng, b, slot):
            for s in range(-5, 2):
                slot(b, 0, s, s)
            with eng.Fori(0, NU - 1) as U:
                for s in range(2, 2 + SPU):
                    slot(b, U, s, None)
            for s in range(2, 2 + SPU):
                slot(b, NU - 1, s, SPU * (NU - 1) + s)

        def walk_f(eng, b, slot):
            for s in range(0, 5):
                slot(b, 0, s, s)
            with eng.Fori(0, NU - 1) as U:
                for s in range(5, 5 + SPU):
                    slot(b, U, s, None)
            for s in range(5, 5 + SPU):
                slot(b, NU - 1, s, SPU * (NU - 1) + s)

        def exists(n, low, high):
            return n is None or low <= n <= high

        @block.sync
        def _(sp):
            sp.dma_start(mask[:, :], causal).then_inc(const_ld, 16)
            sp.dma_start(ident[:, :], eye).then_inc(const_ld, 16)

            with sp.Fori(0, B) as b:
                sp.dma_start(cosb, cos_t.rearrange("p (a t) -> p a t", a=2)).then_inc(tab_ld, 16)
                sp.dma_start(sinb, sin_t.rearrange("p (a t) -> p a t", a=2)).then_inc(tab_ld, 16)
                for k in range(2):
                    sp.dma_start(xt[:, k, :], x[b, k * P:(k + 1) * P, :]).then_inc(ld_x[k], 16)

                def piece_a(i, U, src):
                    prev = i - RING_A
                    slot_ = i % RING_A
                    if isinstance(U, int) and U == 0 and prev < 0:
                        pass
                    else:
                        last = prev - A_PRO
                        if last >= 0:
                            r, u = last, U
                        elif isinstance(U, int) and U == 0:
                            r = None
                            sp.wait_ge(pool_w, b * T_WPOOL_A + prev + 1)
                        else:
                            r, u = last + A_UNIT, U - 1
                        if r is not None:
                            if r == 4:
                                sp.wait_ge(dve_wq0, b * T_WQ0 + u + 1)
                            else:
                                done = r + 1 if r < 4 else r
                                sp.wait_ge(pool_w, b * T_WPOOL_A + A_PRO + 9 * u + done)
                    sp.dma_start(stage[:, slot_, :], src).then_inc(ld_a[slot_], 16)

                for i, src in enumerate([wq[0, 0], wq[0, 1], wq[0, 2], wq[0, 3], wk[0]]):
                    piece_a(i, 0, src)
                with sp.Fori(1, TT // 2) as i:
                    for k in range(2):
                        sp.wait_ge(dve_xn, b * 2 * TT + 2 * i + k - 1)
                        sp.dma_start(xt[:, k, :], x[b, bass.ds((2 * i + k) * P, P), :]).then_inc(ld_x[k], 16)
                piece_a(5, 0, wv[0])

                def unit_a(U, last):
                    for j in range(4):
                        piece_a(A_PRO + j, U, wo[U, j])
                    if not last:
                        for i, src in enumerate([wq[U + 1, 0], wq[U + 1, 1], wq[U + 1, 2], wq[U + 1, 3],
                                                 wk[U + 1], wv[U + 1]]):
                            piece_a(A_PRO + 4 + i, U, src)

                unit_a(0, False)
                with sp.Fori(1, NU - 1) as U:
                    unit_a(U, False)
                unit_a(NU - 1, True)

                for k in range(2):
                    sp.wait_ge(dve_xn, b * 2 * TT + TT - 1 + k)
                    sp.dma_start(xt[:, k, :], x[b, k * P:(k + 1) * P, :]).then_inc(ld_x[k], 16)
                sp.wait_ge(pool_w, b * T_WPOOL_A + T_WPOOL_A)

                def piece_f(i, U, src):
                    slot_ = i % RING_F
                    if not (isinstance(U, int) and U == 0 and i < RING_F):
                        sp.wait_ge(pool_wf, b * T_W_F + F_UNIT * U + i - RING_F + 1)
                    sp.dma_start(stage[:, slot_, :], src).then_inc(ld_f[slot_], 16)

                for j in range(2):
                    piece_f(2 * j, 0, wg[0, j])
                    piece_f(2 * j + 1, 0, wu[0, j])
                with sp.Fori(1, TT // 2) as i:
                    for k in range(2):
                        sp.wait_ge(dve_res, b * TT + 2 * i + k - 1)
                        sp.dma_start(xt[:, k, :], x[b, bass.ds((2 * i + k) * P, P), :]).then_inc(ld_x[k], 16)
                for j in range(2, 4):
                    piece_f(2 * j, 0, wg[0, j])
                    piece_f(2 * j + 1, 0, wu[0, j])

                def unit_f(U, last):
                    for j in range(4):
                        piece_f(F_PRO + j, U, wd[U, j])
                    if not last:
                        for j in range(4):
                            piece_f(F_PRO + 4 + 2 * j, U, wg[U + 1, j])
                            piece_f(F_PRO + 5 + 2 * j, U, wu[U + 1, j])

                with sp.Fori(0, NU - 1) as U:
                    unit_f(U, False)
                unit_f(NU - 1, True)

                with sp.Fori(0, TT // 2) as i:
                    for k in range(2):
                        sp.wait_ge(dve_out, b * TT + 2 * i + k + 1)
                        sp.dma_start(out[b, bass.ds((2 * i + k) * P, P), :], yt[:, k, :]).then_inc(st_out[k], 16)
                for k in range(2):
                    wait_apart(sp, st_out[k], (b + 1) * (TT // 2) * 16)

        @block.tensor
        def _(pe):
            def three(ps, whi, wlo, xhi, xlo, first, last):
                pe.matmul(ps, whi, xhi, start=first, stop=False, skip_group_check=True)
                pe.matmul(ps, wlo, xhi, start=False, stop=False, skip_group_check=True)
                return pe.matmul(ps, whi, xlo, start=False, stop=last, skip_group_check=True)

            def turn(b, layer):
                base = b * 2 * TT + layer * TT
                with pe.Fori(0, TT // 2) as i:
                    for k in range(2):
                        pe.wait_ge(dve_xn, base + 2 * i + k + 1)
                        pe.wait_ge(dve_xl, base + 2 * i + k + 1)
                        for kk in range(KT):
                            ins = pe.transpose(psX[k][:, kk * P:(kk + 1) * P], xn[k][:, kk * P:(kk + 1) * P],
                                               ident[:, :])
                        ins.then_inc(pe_xt, 1)

            def project(ps, w, step):
                for kk in range(KT):
                    ins = three(ps[:, :], Wh[:, w, kk * P:(kk + 1) * P], Wl[:, w, kk * P:(kk + 1) * P],
                                Xh[:, kk, step * W:(step + 1) * W], Xl[:, kk, step * W:(step + 1) * W],
                                kk == 0, kk == KT - 1)
                return ins

            def slot_a(b, U, s, n):
                if exists(n, 0, 31):
                    if s % 4 == 0:
                        need(pe, pool_fl, b, T_ITEM, U, 10, 5 * (s // 4) + 5)
                    need(pe, dve_sf, b, T_SLOT, U, SPU, s)
                    par, c = (s // 4) % 2, s % 4
                    t = slice(c * P, (c + 1) * P)
                    ins = three(psS[:, :].rearrange("p (h t) -> p h t", h=4), Kh[:, t], Kl[:, t],
                                big_h[:, par, :, t], big_l[:, par, :, t], True, True)
                    ins.then_inc(pe_s, 1)
                if exists(n, 1, 32):
                    m = s - 1
                    mu, ms = m // SPU, m % SPU
                    par, c = (m // 4) % 2, m % 4
                    t = slice(c * P, (c + 1) * P)
                    need(pe, pool_sl, b, T_SLOT, U, SPU, m + 1)
                    if c == 0:
                        need(pe, dve_kvl, b, T_KV, U, 4, 2 * (m // 4) + 2)
                    need(pe, dve_a, b, T_SLOT, U, SPU, m)
                    o3 = psO[:, :].rearrange("p (h t) -> p h t", h=4)
                    d3 = psD[:, :].rearrange("p (h t) -> p h t", h=4)
                    first = ms == 0
                    three(o3, Vh[:, c, 0:P], Vl[:, c, :], Sh[:, :, :], Sl[:, :, :], True, first)
                    pe.matmul(d3, ones[:, :], Sh[:, :, :], start=True, stop=False, skip_group_check=True)
                    ins = pe.matmul(d3, ones[:, :], Sl[:, :, :], start=False, stop=first, skip_group_check=True)
                    if not first:
                        need(pe, dve_stl, b, T_STATE, U, 7, 7 * mu + ms)
                        three(o3, Sth[:, 0, :], Stl[:, 0, :], big_h[:, par, :, t], big_l[:, par, :, t], False, True)
                        ins = three(d3, Sth[:, 1, :], Stl[:, 1, :], big_h[:, par, :, t], big_l[:, par, :, t],
                                    False, True)
                    ins.then_inc(pe_pv, 1)
                    if ms < SPU - 1:
                        if first:
                            need(pe, dve_stl, b, T_STATE, U, 7, 7 * mu)
                        pe.matmul(psSt[:, 0:VP], KTh[:, c, :], Vh[:, c, :], start=first, stop=False,
                                  skip_group_check=True)
                        pe.matmul(psSt[:, 0:VP], KTl[:, c, :], Vh[:, c, :], start=False, stop=False,
                                  skip_group_check=True)
                        pe.matmul(psSt[:, 0:P], KTh[:, c, :], Vl[:, c, :], start=False, stop=True,
                                  skip_group_check=True).then_inc(pe_st, 1)
                if s % 4 == 0 and exists(n, 0, 28):
                    need(pe, dve_kvl, b, T_KV, U, 4, 2 * (s // 4))
                    for c in range(4):
                        ins = pe.transpose(psT[:, c * P:(c + 1) * P], kf[:, c * P:(c + 1) * P], ident[:, :])
                    ins.then_inc(pe_tr, 1)
                if exists(n, -5, 26):
                    j = (s + 1) % 4
                    if n is not None and n < -1:
                        pe.wait_ge(pool_w, b * T_WPOOL_A + j + 1)
                    elif s == 3:
                        need(pe, dve_wq0, b, T_WQ0, U, 1, 1)
                    elif 4 <= s <= 6:
                        need(pe, pool_w, b, T_WPOOL_A, U, 9, A_PRO + s + 1)
                    need(pe, dve_t1, b, T_ITEM, U, 10, item_of(s - 1) + 1 if s > -5 else 0)
                    project(psQ, j, ((s + 1) // 4 + 1) % 2).then_inc(pe_q, 1)
                if s % 4 == 2 and exists(n, -2, 26):
                    if n is not None and n < 0:
                        pe.wait_ge(pool_w, b * T_WPOOL_A + 5)
                    elif s == 6:
                        need(pe, pool_w, b, T_WPOOL_A, U, 9, A_PRO + 8)
                    need(pe, act_vt, b, T_STEP, U, 2, (s + 2) // 4)
                    project(psK, 4, ((s + 2) // 4) % 2).then_inc(pe_kv, 1)
                if s % 4 == 3 and exists(n, -1, 27):
                    if n is not None and n < 0:
                        pe.wait_ge(pool_w, b * T_WPOOL_A + 6)
                    elif s == 7:
                        need(pe, pool_w, b, T_WPOOL_A, U, 9, A_PRO + 9)
                    need(pe, dve_t1, b, T_ITEM, U, 10, key_item_of(s - 1) + 1)
                    project(psK, 5, ((s + 1) // 4) % 2).then_inc(pe_kv, 1)
                if s % 4 == 0 and exists(n, 0, 28):
                    need(pe, act_vt, b, T_STEP, U, 2, s // 4 + 1)
                    need(pe, dve_kvl, b, T_KV, U, 4, 2 * (s // 4) + 1)
                    for c in range(4):
                        ins = pe.transpose(psT[:, c * P:(c + 1) * P], vT[:, c * P:(c + 1) * P], ident[:, :])
                    ins.then_inc(pe_tr, 1)
                if exists(n, 2, 33):
                    need(pe, pool_al, b, T_SLOT, U, SPU, s - 1)
                    need(pe, dve_y, b, T_SLOT + 1, U, SPU, s - 1)
                    for h in range(4):
                        if s == 2:
                            need(pe, pool_w, b, T_WPOOL_A, U, 9, A_PRO + h + 1)
                        ins = three(psY[:, :], Ah[:, h, :], Al[:, h, :], Oh[:, h, :], Ol[:, h, :], h == 0, h == 3)
                    ins.then_inc(pe_y, 1)

            def slot_f(b, U, s, n):
                j = s % 4
                if exists(n, 0, 31):
                    if n is not None and n < 4:
                        pe.wait_ge(pool_wf, b * T_W_F + 2 * j + 2)
                    elif s >= 8 and s < 12:
                        need(pe, pool_wf, b, T_W_F, U, F_UNIT, F_PRO + 4 + 2 * j + 2)
                    need(pe, act_sg, b, T_SLOT, U, SPU, s - 1)
                    project(psG[s % 2], j, (s // 4) % 2).then_inc(pe_g, 1)
                    need(pe, dve_h, b, T_SLOT, U, SPU, s - 1)
                    project(psU[s % 2], 4 + j, (s // 4) % 2).then_inc(pe_u, 1)
                if exists(n, 5, 36):
                    y = s - 5
                    d, ts = y // 4, y % 4
                    need(pe, dve_yf, b, T_SLOT + 2, U, SPU, y + 1)
                    for i in range(4):
                        if ts == 0 and i < 2:
                            need(pe, pool_hl, b, 4 * NU, U, 4, 2 * d + i + 1)
                        elif ts == 0:
                            need(pe, dve_hl, b, 4 * NU, U, 4, 2 * d + i - 1)
                        if s == 5:
                            need(pe, pool_wf, b, T_W_F, U, F_UNIT, F_PRO + i + 1)
                        ins = three(psYF[y % 2][:, :], big_h[:, d % 2, i, ts * P:(ts + 1) * P],
                                    big_l[:, d % 2, i, ts * P:(ts + 1) * P], Oh[:, i, :], Ol[:, i, :],
                                    i == 0, i == 3)
                    ins.then_inc(pe_d, 1)

            pe.wait_ge(const_ok, 1)
            with pe.Fori(0, B) as b:
                turn(b, 0)
                pe.wait_ge(dve_xl, 2 + b * 2 * TT + TT)
                walk_a(pe, b, slot_a)
                turn(b, 1)
                pe.wait_ge(dve_xl, 2 + b * 2 * TT + 2 * TT)
                walk_f(pe, b, slot_f)

        @block.scalar
        def _(act):
            copy = nc.scalar.copy

            def split_x(b, layer, pieces):
                base = b * 2 * TT + layer * TT
                for i in range(TT // 2):
                    for k in range(2):
                        act.wait_ge(pe_xt, base + 2 * i + k + 1)
                        t = (2 * i + k) * P
                        copy(Xh[:, :, t:t + P],
                             psX[k][:, :].rearrange("p (c t) -> p c t", c=KT)).then_inc(act_xh, 1)
                    for piece in pieces[i]:
                        (wsplit_f if layer else wsplit_a)(b, 0, piece, Wh[:, first_unit[layer][piece], :])

            def raw(b, ring, lds, i, U, per_unit, total):
                slot_ = i % ring
                k = i // ring + 1
                act.wait_ge(lds[slot_], (b * total + U * (per_unit // ring) + k) * 16)
                return stage[:, slot_, :]

            def count_a(slot_):
                return sum(1 for i in range(T_WACT_A) if i % RING_A == slot_)

            def count_f(slot_):
                return sum(1 for i in range(T_W_F) if i % RING_F == slot_)

            def wsplit_a(b, U, i, dst):
                copy(dst, raw(b, RING_A, ld_a, i, U, A_UNIT, count_a(i % RING_A))).then_inc(act_w, 1)

            def wsplit_f(b, U, i, dst):
                copy(dst, raw(b, RING_F, ld_f, i, U, F_UNIT, count_f(i % RING_F))).then_inc(act_wf, 1)

            def turn_half(src):
                def to(dst):
                    copy(dst[HALF:P, :], src[0:HALF, :])
                    return copy(dst[0:HALF, :], src[HALF:P, :])
                return to

            def slot_a(b, U, s, n):
                if s == 2 and exists(n, 2, 26):
                    need(act, pe_s, b, T_SLOT, U, SPU, s + 1)
                    for h in range(4):
                        wsplit_a(b, U, A_PRO + h, Oh[:, h, :])
                    if exists(n, 2, 25):
                        need(act, pe_q, b, T_SLOT, U, SPU, 5)
                        wsplit_a(b, U, A_PRO + 4, Wh[:, 0, :])
                if s == 3 and exists(n, 2, 25):
                    need(act, pe_q, b, T_SLOT, U, SPU, 7)
                    wsplit_a(b, U, A_PRO + 5, Wh[:, 1, :])
                    wsplit_a(b, U, A_PRO + 6, Wh[:, 2, :])
                if s == 4 and exists(n, 2, 25):
                    need(act, pe_q, b, T_SLOT, U, SPU, 8)
                    wsplit_a(b, U, A_PRO + 7, Wh[:, 3, :])
                    need(act, pe_kv, b, T_KV, U, 4, 3)
                    wsplit_a(b, U, A_PRO + 8, Wh[:, 4, :])
                if s == 5 and exists(n, 2, 25):
                    need(act, pe_kv, b, T_KV, U, 4, 4)
                    wsplit_a(b, U, A_PRO + 9, Wh[:, 5, :])
                if exists(n, 2, 33):
                    need(act, dve_a, b, T_SLOT, U, SPU, s - 1)
                    if n is None or n <= 31:
                        need(act, pe_s, b, T_SLOT, U, SPU, s + 1)
                    else:
                        need(act, pe_y, b, T_SLOT, U, SPU, s - 2)
                    copy(Ah[:, :, :].rearrange("p h t -> p (h t)"), of).then_inc(act_ah, 1)
                m = s - 1
                it = item_of(m)
                q_item = exists(n, -4, 27)
                k_item = m % 4 == 2 and exists(n, -1, 27)
                if q_item:
                    need(act, pe_q, b, T_SLOT, U, SPU, m + 6)
                    need(act, dve_x, b, T_ITEM, U, 10, it)
                    turn_half(psQ)(rot).then_inc(act_rot, 1)
                if k_item:
                    need(act, pe_kv, b, T_KV, U, 4, 2 * ((s + 1) // 4) + 1)
                    need(act, pe_tr, b, T_KV, U, 4, 2 * ((s + 1) // 4))
                    turn_half(psK)(vT).then_inc(act_rot, 1)
                if s % 4 == 0 and exists(n, 0, 28):
                    need(act, pe_kv, b, T_KV, U, 4, 2 * (s // 4) + 2)
                    need(act, dve_x, b, T_ITEM, U, 10, key_item_of(s - 2) + 1)
                    copy(vT, psK[:, :]).then_inc(act_vt, 1)
                if exists(n, 1, 32):
                    need(act, pe_pv, b, T_SLOT, U, SPU, s)
                    need(act, dve_U, b, T_SLOT, U, SPU, s - 1)
                    nc.scalar.activation(r0, psD[:, :], ACT.Ln, bias=eps_den[:, 0:1]).then_inc(act_ln, 1)
                if q_item:
                    need(act, dve_x, b, T_ITEM, U, 10, it + 1)
                    nc.scalar.activation(Eq, xq, ACT.Exp).then_inc(act_exp, 1)
                if exists(n, 1, 32):
                    need(act, act_ln, b, T_SLOT, U, SPU, s)
                    nc.scalar.activation(r0, r0, ACT.Exp, scale=-1.0).then_inc(act_r0, 1)
                if k_item:
                    need(act, dve_x, b, T_ITEM, U, 10, it + 2)
                    nc.scalar.activation(Ek, xk, ACT.Exp).then_inc(act_exp, 1)
                if s % 4 == 0 and exists(n, 0, 28):
                    need(act, pe_tr, b, T_KV, U, 4, 2 * (s // 4) + 1)
                    copy(KTh[:, :, :].rearrange("p c d -> p (c d)"), psT[:, :]).then_inc(act_kvh, 1)
                if exists(n, 0, 31):
                    need(act, dve_sf, b, T_SLOT, U, SPU, s + 1)
                    need(act, pe_pv, b, T_SLOT, U, SPU, s)
                    copy(Sh[:, :, :].rearrange("p h t -> p (h t)"), Sf).then_inc(act_sh, 1)
                mu, ms = m // SPU, m % SPU
                if exists(n, 1, 32) and ms < SPU - 1:
                    need(act, pe_st, b, T_STATE, U, 7, 7 * mu + ms + 1)
                    copy(Sth[:, 0, :], psSt[:, 0:P])
                    copy(Sth[:, 1, :], psSt[:, P:P + 1].to_broadcast([P, P])).then_inc(act_sth, 1)
                if s % 4 == 0 and exists(n, 0, 28):
                    need(act, pe_tr, b, T_KV, U, 4, 2 * (s // 4) + 2)
                    copy(Vh[:, :, 0:P], psT[:, :].rearrange("p (c d) -> p c d", c=4)).then_inc(act_kvh, 1)
                if q_item:
                    need(act, dve_f, b, T_ITEM, U, 10, it + 1)
                    if m >= 3 or n is None:
                        need(act, pe_pv, b, T_SLOT, U, SPU, s)
                    copy(big_h[:, ((m + 1) // 4 + 1) % 2, (m + 1) % 4, :], fq).then_inc(act_fh, 1)
                if k_item:
                    need(act, dve_f, b, T_ITEM, U, 10, it + 2)
                    if m >= 2:
                        need(act, pe_s, b, T_SLOT, U, SPU, s + 1)
                    copy(Kh[:, :], kf).then_inc(act_fh, 1)

            def slot_f(b, U, s, n):
                j = s % 4
                if s == 5 and exists(n, 5, 29):
                    need(act, pe_g, b, T_SLOT, U, SPU, s + 1)
                    for i in range(4):
                        wsplit_f(b, U, F_PRO + i, Oh[:, i, :])
                if 5 <= s <= 8 and exists(n, 5, 28):
                    i = s - 5
                    need(act, pe_u, b, T_SLOT, U, SPU, s)
                    wsplit_f(b, U, F_PRO + 4 + 2 * i, Wh[:, i, :])
                    wsplit_f(b, U, F_PRO + 5 + 2 * i, Wh[:, 4 + i, :])
                if exists(n, 1, 32):
                    i = (s - 1) % 4
                    need(act, dve_h, b, T_SLOT, U, SPU, s)
                    need(act, dve_rank, b, T_STEP, U, 2, (s - 1) // 4)
                    nc.scalar.activation(ab[:, i, :], hid[:, i, :], ACT.Abs).then_inc(act_ab, 1)
                if exists(n, 0, 31):
                    need(act, pe_g, b, T_SLOT, U, SPU, s + 1)
                    need(act, dve_h, b, T_SLOT, U, SPU, s)
                    nc.scalar.activation(sg, psG[s % 2][:, :], ACT.Silu).then_inc(act_sg, 1)
                if j == 0 and exists(n, 4, 32):
                    d = s // 4 - 1
                    for i in range(4):
                        need(act, dve_hs, b, 8 * NU, U, 8, 4 * d + i + 1)
                        copy(big_h[:, d % 2, i, :], hid[:, i, :]).then_inc(act_hh, 1)

            act.wait_ge(const_ok, 1)
            with act.Fori(0, B) as b:
                nc.scalar.preload_act_table_set("natural_log_exp_and_others")
                split_x(b, 0, pieces_a)
                walk_a(act, b, slot_a)
                split_x(b, 1, pieces_f)
                walk_f(act, b, slot_f)

        @block.vector
        def _(dve):
            def layernorm_rows(b, layer):
                base = b * 2 * TT + layer * TT
                with dve.Fori(0, TT // 2) as i:
                    srcs = []
                    for k in range(2):
                        srcs.append(xt[:, k, :] if layer == 0 else Y[:, 2 * i + k, :])
                    if layer == 1:
                        rsb = b * 4 * TT + TT + 4 * i
                        se = b * SELF + SELF_LN0 + 6 * i
                        for k in range(2):
                            dve.bn_stats(stat[:, k, :], srcs[k]).then_inc(dve_self, 1)
                        for k in range(2):
                            wait_apart(dve, dve_self, se + k + 1)
                            dve.bn_aggr(mv[:, k, :], stat[:, k, :]).then_inc(ln_var, 1)
                        for k in range(2):
                            dve.wait_ge(pool_rs, rsb + k + 1)
                            dve.wait_ge(ln_var, rsb + k + 1)
                            dve.tensor_scalar(Y[:, 2 * i + k, :], Y[:, 2 * i + k, :], mv[:, k, 0:1],
                                              rstd[:, k:k + 1], ALU.subtract, ALU.mult).then_inc(dve_self, 1)
                        for k in range(2):
                            dve.wait_ge(dve_self, se + 2 + k + 1)
                            dve.wait_ge(ld_x[k], (b * TT + TT // 2 + i + 1) * 16)
                            dve.tensor_tensor(Y[:, 2 * i + k, :], Y[:, 2 * i + k, :], xt[:, k, :],
                                              ALU.add).then_inc(dve_res, 1)
                        for k in range(2):
                            wait_apart(dve, dve_res, b * TT + 2 * i + k + 1)
                            dve.bn_stats(stat[:, k, :], srcs[k]).then_inc(dve_self, 1)
                        rsb2 = rsb + 2
                        se2 = se + 4
                    else:
                        rsb2 = b * 4 * TT + 2 * i
                        se2 = b * SELF + 2 * i
                        for k in range(2):
                            wait_apart(dve, ld_x[k], (b * TT + i + 1) * 16)
                            dve.bn_stats(stat[:, k, :], srcs[k]).then_inc(dve_self, 1)
                    for k in range(2):
                        wait_apart(dve, dve_self, se2 + k + 1)
                        dve.bn_aggr(mv[:, k, :], stat[:, k, :]).then_inc(ln_var, 1)
                    for k in range(2):
                        dve.wait_ge(pool_rs, rsb2 + k + 1)
                        dve.wait_ge(ln_var, rsb2 + k + 1)
                        dve.tensor_scalar(xn[k], srcs[k], mv[:, k, 0:1], rstd[:, k:k + 1],
                                          ALU.subtract, ALU.mult).then_inc(dve_xn, 1)
                    for k in range(2):
                        dve.wait_ge(act_xh, base + 2 * i + k + 1)
                        dve.tensor_tensor(Xl[:, :, bass.ds((2 * i + k) * P, P)],
                                          psX[k][:, :].rearrange("p (c t) -> p c t", c=KT),
                                          Xh[:, :, bass.ds((2 * i + k) * P, P)].bitcast(F32),
                                          ALU.subtract).then_inc(dve_xl, 1)

            def slot_a(b, U, s, n):
                m = s - 1
                it = item_of(m)
                mu, ms = m // SPU, m % SPU
                q_item = exists(n, -4, 27)
                k_item = m % 4 == 2 and exists(n, -1, 27)
                pstep = ((m + 1) // 4 + 1) % 2
                if exists(n, 0, 31):
                    need(dve, pe_s, b, T_SLOT, U, SPU, s + 1)
                    need(dve, pool_sl, b, T_SLOT, U, SPU, s)
                    dve.tensor_tensor(Sf.rearrange("p (h t) -> p h t", h=4),
                                      psS[:, :].rearrange("p (h t) -> p h t", h=4),
                                      mask[:, :].rearrange("p (o t) -> p o t", o=1).to_broadcast([P, 4, P]),
                                      ALU.mult).then_inc(dve_sf, 1)
                if q_item:
                    need(dve, act_rot, b, T_ITEM, U, 10, it + 1)
                    dve.tensor_tensor(xq, psQ[:, :], cosb[:, pstep, :], ALU.mult).then_inc(dve_t1, 1)
                    dve.tensor_tensor(rot, rot, sinb[:, pstep, :], ALU.mult).then_inc(dve_t2, 1)
                if k_item:
                    kstep = ((s + 1) // 4) % 2
                    need(dve, act_rot, b, T_ITEM, U, 10, it + 2)
                    dve.tensor_tensor(xk, psK[:, :], cosb[:, kstep, :], ALU.mult).then_inc(dve_t1, 1)
                    dve.tensor_tensor(vT, vT, sinb[:, kstep, :], ALU.mult).then_inc(dve_t2, 1)
                if q_item:
                    need(dve, dve_t2, b, T_ITEM, U, 10, it + 1)
                    dve.tensor_tensor(xq, xq, rot, ALU.add).then_inc(dve_x, 1)
                if k_item:
                    need(dve, dve_t2, b, T_ITEM, U, 10, it + 2)
                    dve.tensor_tensor(xk, xk, vT, ALU.add).then_inc(dve_x, 1)
                if exists(n, 1, 32):
                    need(dve, act_r0, b, T_SLOT, U, SPU, s)
                    dve.scalar_tensor_tensor(Tn, psD[:, :], EPS_DEN, r0, ALU.add, ALU.mult).then_inc(dve_T, 1)
                if q_item:
                    need(dve, act_exp, b, T_ITEM, U, 10, it + 1)
                    dve.tensor_scalar(Eq, Eq, 1.0, None, ALU.min).then_inc(dve_m, 1)
                if exists(n, 1, 32):
                    need(dve, dve_T, b, T_SLOT, U, SPU, s)
                    dve.scalar_tensor_tensor(Tn, Tn, 2.0, r0, ALU.subtract, ALU.mult).then_inc(dve_U, 1)
                if q_item:
                    need(dve, dve_m, b, T_ITEM, U, 10, it + 1)
                    need(dve, pool_fl, b, T_ITEM, U, 10, it)
                    dve.scalar_tensor_tensor(fq, xq, 0.0, Eq, ALU.max, ALU.add).then_inc(dve_f, 1)
                if k_item:
                    need(dve, act_exp, b, T_ITEM, U, 10, it + 2)
                    dve.tensor_scalar(Ek, Ek, 1.0, None, ALU.min).then_inc(dve_m, 1)
                if exists(n, 1, 32):
                    need(dve, dve_U, b, T_SLOT, U, SPU, s)
                    need(dve, pool_al, b, T_SLOT, U, SPU, m)
                    dve.scalar_tensor_tensor(of, Tn, -1.0, psO[:, :], ALU.mult, ALU.mult).then_inc(dve_a, 1)
                if k_item:
                    need(dve, dve_m, b, T_ITEM, U, 10, it + 2)
                    dve.scalar_tensor_tensor(kf, xk, 0.0, Ek, ALU.max, ALU.add).then_inc(dve_f, 1)
                if s % 4 == 0 and exists(n, 0, 28):
                    need(dve, act_kvh, b, T_KV, U, 4, 2 * (s // 4) + 1)
                    dve.tensor_tensor(KTl[:, :, :].rearrange("p c d -> p (c d)"), psT[:, :],
                                      KTh[:, :, :].rearrange("p c d -> p (c d)").bitcast(F32), ALU.subtract).then_inc(dve_kvl, 1)
                if exists(n, 1, 32) and ms < SPU - 1:
                    need(dve, act_sth, b, T_STATE, U, 7, 7 * mu + ms + 1)
                    dve.tensor_tensor(Stl[:, 0, :], psSt[:, 0:P], Sth[:, 0, :].bitcast(F32), ALU.subtract)
                    dve.tensor_tensor(Stl[:, 1, :], psSt[:, P:P + 1].to_broadcast([P, P]),
                                      Sth[:, 1, :].bitcast(F32), ALU.subtract).then_inc(dve_stl, 1)
                if s % 4 == 0 and exists(n, 0, 28):
                    need(dve, act_kvh, b, T_KV, U, 4, 2 * (s // 4) + 2)
                    dve.tensor_tensor(Vl[:, :, :], psT[:, :].rearrange("p (c d) -> p c d", c=4),
                                      Vh[:, :, 0:P].bitcast(F32), ALU.subtract).then_inc(dve_kvl, 1)
                if s == 2 and exists(n, 2, 25):
                    need(dve, act_w, b, T_WACT_A, U, A_UNIT, A_PRO + 5)
                    dve.tensor_tensor(Wl[:, 0, :], stage[:, (A_PRO + 4) % RING_A, :],
                                      Wh[:, 0, :].bitcast(F32), ALU.subtract).then_inc(dve_wq0, 1)
                if n == -5:
                    dve.memset(Y[:, :, :], 0.0).then_inc(dve_y, 1)
                if exists(n, 2, 33):
                    need(dve, pe_y, b, T_SLOT, U, SPU, s - 1)
                    t = (s - 2) % SPU
                    dve.tensor_tensor(Y[:, t, :], psY[:, :], Y[:, t, :], ALU.add).then_inc(dve_y, 1)

            def slot_f(b, U, s, n):
                if exists(n, 1, 32):
                    i = (s - 1) % 4
                    need(dve, pe_u, b, T_SLOT, U, SPU, s)
                    need(dve, act_sg, b, T_SLOT, U, SPU, s)
                    if s >= 5:
                        d = (s - 1) // 4 - 1
                        if i < 2:
                            need(dve, pool_hl, b, 4 * NU, U, 4, 2 * d + i + 1)
                        else:
                            need(dve, dve_hl, b, 4 * NU, U, 4, 2 * d + i - 1)
                    dve.tensor_tensor(hid[:, i, :], psU[(s - 1) % 2][:, :], sg, ALU.mult).then_inc(dve_h, 1)
                def pair(i, c, steps):
                    need(dve, act_ab, b, T_SLOT, U, SPU, steps)
                    dve.tensor_tensor(c, ab[:, 2 * i, :], ab[:, 2 * i + 1, :], ALU.is_ge)
                    dve.tensor_tensor(Wmax[:, i, :], ab[:, 2 * i, :], ab[:, 2 * i + 1, :], ALU.max)
                    return dve.tensor_tensor(ab[:, 2 * i, :], ab[:, 2 * i, :], ab[:, 2 * i + 1, :], ALU.min)

                if s % 4 == 3 and exists(n, 3, 31):
                    pair(0, c01, s - 1).then_inc(dve_self, 1)
                if s % 4 == 0 and exists(n, 4, 32):
                    d = s // 4 - 1
                    pair(1, c23, s).then_inc(dve_self, 1)
                    sb_, per = SELF_F0, 2 * SELF_F
                    k0 = d * SELF_F + sb_

                    def own(k):
                        need(dve, dve_self, b, SELF, U, per, k0 + k)

                    own(2)
                    dve.tensor_tensor(pw, ab[:, 0, :], Wmax[:, 1, :], ALU.is_ge).then_inc(dve_self, 1)
                    dve.tensor_tensor(qw, ab[:, 2, :], Wmax[:, 0, :], ALU.is_gt).then_inc(dve_rank, 1)
                    own(3)
                    need(dve, dve_rank, b, T_STEP, U, 2, d + 1)
                    dve.tensor_tensor(rr, qw, pw, ALU.subtract).then_inc(dve_self, 1)
                    dve.tensor_tensor(pw, pw, qw, ALU.subtract).then_inc(dve_self, 1)
                    own(4)
                    dve.tensor_tensor(m0, c01, rr, ALU.is_gt).then_inc(dve_self, 1)
                    own(5)
                    dve.tensor_tensor(m2, c23, pw, ALU.is_gt).then_inc(dve_self, 1)
                    dve.tensor_scalar(rr, rr, -1.0, 1.0, ALU.mult, ALU.add).then_inc(dve_self, 1)
                    dve.tensor_scalar(pw, pw, -1.0, 1.0, ALU.mult, ALU.add).then_inc(dve_self, 1)
                    own(6)
                    dve.tensor_tensor(hid[:, 0, :], hid[:, 0, :], m0, ALU.mult).then_inc(dve_hs, 1)
                    own(8)
                    dve.tensor_tensor(c01, c01, rr, ALU.is_lt).then_inc(dve_self, 1)
                    own(9)
                    dve.tensor_tensor(c23, c23, pw, ALU.is_lt).then_inc(dve_self, 1)
                    own(10)
                    dve.tensor_tensor(hid[:, 1, :], hid[:, 1, :], c01, ALU.mult).then_inc(dve_hs, 1)
                    own(7)
                    dve.tensor_tensor(hid[:, 2, :], hid[:, 2, :], m2, ALU.mult).then_inc(dve_hs, 1)
                    own(11)
                    dve.tensor_tensor(hid[:, 3, :], hid[:, 3, :], c23, ALU.mult).then_inc(dve_hs, 1)
                    for i in range(2, 4):
                        need(dve, act_hh, b, 8 * NU, U, 8, 4 * d + i + 1)
                        dve.tensor_tensor(big_l[:, d % 2, i, :], hid[:, i, :], big_h[:, d % 2, i, :].bitcast(F32),
                                          ALU.subtract).then_inc(dve_hl, 1)
                if n == 1:
                    dve.memset(YF, 0.0).then_inc(dve_yf, 2)
                if exists(n, 5, 36):
                    y = s - 5
                    need(dve, pe_d, b, T_SLOT, U, SPU, y + 1)
                    t = y % TT
                    dve.tensor_tensor(YF[:, t, :], psYF[y % 2][:, :], YF[:, t, :], ALU.add).then_inc(dve_yf, 1)

            def finish(b):
                def pair_of_tiles(i, stores_before):
                    rsb = b * 4 * TT + 3 * TT + 2 * i
                    se = b * SELF + SELF_END + 4 * i
                    for k in range(2):
                        dve.bn_stats(stat[:, k, :], YF[:, 2 * i + k, :]).then_inc(dve_self, 1)
                    for k in range(2):
                        wait_apart(dve, dve_self, se + k + 1)
                        dve.bn_aggr(mv[:, k, :], stat[:, k, :]).then_inc(ln_var, 1)
                    for k in range(2):
                        dve.wait_ge(pool_rs, rsb + k + 1)
                        dve.wait_ge(ln_var, rsb + k + 1)
                        dve.tensor_scalar(YF[:, 2 * i + k, :], YF[:, 2 * i + k, :], mv[:, k, 0:1],
                                          rstd[:, k:k + 1], ALU.subtract, ALU.mult).then_inc(dve_self, 1)
                    for k in range(2):
                        dve.wait_ge(dve_self, se + 2 + k + 1)
                        if stores_before:
                            dve.wait_ge(st_out[k], (b * (TT // 2) + i) * 16)
                        dve.tensor_tensor(yt[:, k, :], YF[:, 2 * i + k, :], Y[:, 2 * i + k, :],
                                          ALU.add).then_inc(dve_out, 1)

                pair_of_tiles(0, False)
                with dve.Fori(1, TT // 2) as i:
                    pair_of_tiles(i, True)

            SELF_LN0 = 2 * (TT // 2)
            SELF_F0 = SELF_LN0 + 6 * (TT // 2)
            SELF_F = 11
            SELF_END = SELF_F0 + SELF_F * T_STEP
            SELF = SELF_END + 4 * (TT // 2)

            dve.memset(eps_den[:, :], EPS_DEN)
            dve.memset(mhalf[:, :], -0.5)
            dve.memset(eps_ln[:, :], EPS_LN)
            dve.memset(Sf, 1.0).then_inc(dve_const, 1)
            dve.memset(r0, 0.0).then_inc(dve_const, 1)
            dve.wait_ge(dve_const, 2)
            dve.tensor_copy(ones[:, :], Sf[:, 0:P])
            dve.tensor_copy(Vh[:, :, P:P + 1], Sf[:, 0:4].rearrange("p (c o) -> p c o", o=1))
            dve.tensor_copy(Vh[:, :, P + 1:P + 2], r0[:, 0:4].rearrange("p (c o) -> p c o", o=1))
            dve.wait_ge(const_ld, 32)
            dve.memset(rstd[:, :], 0.0).then_inc(const_ok, 1)
            dve.memset(mv[:, :, :], 0.0).then_inc(dve_xl, 2)
            with dve.Fori(0, B) as b:
                layernorm_rows(b, 0)
                dve.wait_ge(tab_ld, b * 32 + 32)
                walk_a(dve, b, slot_a)
                layernorm_rows(b, 1)
                walk_f(dve, b, slot_f)
                finish(b)

        @block.gpsimd
        def _(pool):
            def lo(dst, full, hi):
                return pool.tensor_tensor(dst, full, hi.bitcast(F32), ALU.subtract)

            def deviations(b, k):
                pool.wait_ge(ln_var, b * 4 * TT + k + 2)
                pool.tensor_tensor(rstd[:, :], mv[:, :, 1], eps_ln[:, :], ALU.add).then_inc(pool_eps, 1)
                pool.wait_ge(pool_eps, b * 2 * TT + k // 2 + 1)
                pool.tensor_tensor(rstd[:, :], rstd[:, :], mhalf[:, :], ALU.pow).then_inc(pool_rs, 2)

            def wlo_a(b, U, i, dst, hi):
                need(pool, act_w, b, T_WACT_A, U, A_UNIT, i + 1)
                lo(dst, stage[:, i % RING_A, :], hi).then_inc(pool_w, 1)

            def wlo_f(b, U, i, dst, hi):
                need(pool, act_wf, b, T_W_F, U, F_UNIT, i + 1)
                lo(dst, stage[:, i % RING_F, :], hi).then_inc(pool_wf, 1)

            def slot_a(b, U, s, n):
                m = s - 1
                it = item_of(m)
                if exists(n, 2, 33):
                    need(pool, act_ah, b, T_SLOT, U, SPU, s - 1)
                    lo(Al[:, :, :].rearrange("p h t -> p (h t)"), of,
                       Ah[:, :, :].rearrange("p h t -> p (h t)")).then_inc(pool_al, 1)
                if s == 2 and exists(n, 2, 26):
                    for h in range(4):
                        wlo_a(b, U, A_PRO + h, Ol[:, h, :], Oh[:, h, :])
                if s == 3 and exists(n, 2, 25):
                    wlo_a(b, U, A_PRO + 5, Wl[:, 1, :], Wh[:, 1, :])
                    wlo_a(b, U, A_PRO + 6, Wl[:, 2, :], Wh[:, 2, :])
                if s == 4 and exists(n, 2, 25):
                    wlo_a(b, U, A_PRO + 7, Wl[:, 3, :], Wh[:, 3, :])
                    wlo_a(b, U, A_PRO + 8, Wl[:, 4, :], Wh[:, 4, :])
                if s == 5 and exists(n, 2, 25):
                    wlo_a(b, U, A_PRO + 9, Wl[:, 5, :], Wh[:, 5, :])
                if exists(n, 0, 31):
                    need(pool, act_sh, b, T_SLOT, U, SPU, s + 1)
                    lo(Sl[:, :, :].rearrange("p h t -> p (h t)"), Sf,
                       Sh[:, :, :].rearrange("p h t -> p (h t)")).then_inc(pool_sl, 1)
                if exists(n, -4, 27):
                    par, h = ((m + 1) // 4 + 1) % 2, (m + 1) % 4
                    need(pool, act_fh, b, T_ITEM, U, 10, it + 1)
                    lo(big_l[:, par, h, :], fq, big_h[:, par, h, :]).then_inc(pool_fl, 1)
                if m % 4 == 2 and exists(n, -1, 27):
                    need(pool, act_fh, b, T_ITEM, U, 10, it + 2)
                    lo(Kl[:, :], kf, Kh[:, :]).then_inc(pool_fl, 1)

            def slot_f(b, U, s, n):
                if s % 4 == 0 and exists(n, 4, 32):
                    d = s // 4 - 1
                    for i in range(2):
                        need(pool, act_hh, b, 8 * NU, U, 8, 4 * d + i + 1)
                        lo(big_l[:, d % 2, i, :], hid[:, i, :], big_h[:, d % 2, i, :]).then_inc(pool_hl, 1)
                if s == 5 and exists(n, 5, 29):
                    for i in range(4):
                        wlo_f(b, U, F_PRO + i, Ol[:, i, :], Oh[:, i, :])
                if 5 <= s <= 8 and exists(n, 5, 28):
                    i = s - 5
                    wlo_f(b, U, F_PRO + 4 + 2 * i, Wl[:, i, :], Wh[:, i, :])
                    wlo_f(b, U, F_PRO + 5 + 2 * i, Wl[:, 4 + i, :], Wh[:, 4 + i, :])

            pool.wait_ge(const_ok, 1)
            with pool.Fori(0, B) as b:
                for i in range(TT // 2):
                    deviations(b, 2 * i)
                    for piece in pieces_a[i]:
                        w = first_unit[0][piece]
                        wlo_a(b, 0, piece, Wl[:, w, :], Wh[:, w, :])
                walk_a(pool, b, slot_a)
                for i in range(TT // 2):
                    deviations(b, TT + 4 * i)
                    deviations(b, TT + 4 * i + 2)
                    for piece in pieces_f[i]:
                        w = first_unit[1][piece]
                        wlo_f(b, 0, piece, Wl[:, w, :], Wh[:, w, :])
                walk_f(pool, b, slot_f)
                for i in range(TT // 2):
                    deviations(b, 3 * TT + 2 * i)


_OUT = ((B, S, DM), "float32")


def kernel(L0_attn_x, L0_attn_Wq, L0_attn_Wk, L0_attn_Wv, L0_attn_Wo,
           L0_ffn_w_gate, L0_ffn_w_up, L0_ffn_w_down):
    import concourse.bacc as bacc
    from concourse.bass_utils import run_bass_kernel_spmd

    def f(a):
        return np.ascontiguousarray(a)

    Wq = np.asarray(L0_attn_Wq).reshape(KVH, REP, P, KT, P).transpose(0, 1, 4, 3, 2)
    Wk = np.asarray(L0_attn_Wk).reshape(KVH, P, KT, P).transpose(0, 3, 2, 1)
    Wv = np.asarray(L0_attn_Wv).reshape(KVH, P, KT, P).transpose(0, 3, 2, 1)
    Wo = np.asarray(L0_attn_Wo).reshape(DM, KVH, REP, P).transpose(1, 2, 3, 0)
    Wg = np.asarray(L0_ffn_w_gate).reshape(KT, P, NU, P, 4).transpose(2, 4, 1, 0, 3)
    Wu = np.asarray(L0_ffn_w_up).reshape(KT, P, NU, P, 4).transpose(2, 4, 1, 0, 3)
    Wd = np.asarray(L0_ffn_w_down).reshape(NU, P, 4, DM).transpose(0, 2, 1, 3)
    power = np.arange(0, P, 2, dtype=np.float32) / np.float32(P)
    freq = np.float32(1) / np.power(10000.0, power.astype(np.float64)).astype(np.float32)
    angle = np.outer(freq, np.arange(S, dtype=np.float32)).astype(np.float64)
    cos = np.cos(angle).astype(np.float32)
    sin = np.sin(angle).astype(np.float32)
    place = np.arange(P)
    arrays = {
        "x": f(L0_attn_x),
        "wq": f(Wq).reshape(NU, 4, P, W), "wk": f(Wk).reshape(NU, P, W), "wv": f(Wv).reshape(NU, P, W),
        "wo": f(Wo), "wg": f(Wg).reshape(NU, 4, P, W), "wu": f(Wu).reshape(NU, 4, P, W), "wd": f(Wd),
        "cos_t": np.concatenate([cos, cos]), "sin_t": np.concatenate([-sin, sin]),
        "causal": (place[:, None] <= place[None, :]).astype(np.float32),
        "eye": np.eye(P, dtype=np.float32),
    }
    nc = bacc.Bacc("TRN2", target_bir_lowering=False, num_devices=1)
    args = [nc.dram_tensor(n, a.shape, mybir.dt.from_np(a.dtype), kind="ExternalInput").ap()
            for n, a in arrays.items()]
    shape, dtype = _OUT
    args.append(nc.dram_tensor("out", shape, mybir.dt.from_np(np.dtype(dtype)), kind="ExternalOutput").ap())
    build(nc, *args)
    r = run_bass_kernel_spmd(nc, [arrays], core_ids=[0])
    return r.results[0]["out"]
```

```python
from contextlib import ExitStack

import numpy as np

import concourse.bass as bass
from concourse import mybir

ALU = mybir.AluOpType
ACT = mybir.ActivationFunctionType
F32 = mybir.dt.float32
F32R = mybir.dt.float32r
BF16 = mybir.dt.bfloat16

P = 128
B, S, DM = 2, 1024, 512
KVH, REP = 4, 4
W = 512
KT = DM // P
TT = S // P
HALF = P // 2
NU = 4
SPU = 8
EPS_LN = 1e-5
EPS_DEN = 1e-6
VP = P + 2

RING_A, RING_F = 5, 4
A_PRO, A_UNIT = 6, 10
F_PRO, F_UNIT = 8, 12

T_SLOT = NU * SPU
T_ITEM = 5 * 2 * NU
T_KV = 2 * 2 * NU
T_STEP = 2 * NU
T_STATE = 7 * NU
W_DVE = {0: 1, 1: 2, 4: 3}
W_POOL = {2: 1, 3: 2, 5: 3, 6: 4, 7: 5, 8: 6, 9: 7}
T_WPOOL_A = A_PRO + len(W_POOL) * (NU - 1) + 2
T_WDVE = len(W_DVE) * (NU - 1) + 2
T_WACT_A = A_PRO + 10 * (NU - 1) + 4
T_W_F = F_PRO + F_UNIT * (NU - 1) + 4


KINDS = ("in", "mid", "out")


def jobs(b, layer, n):
    if n is None:
        return []
    found = []
    if layer == 0:
        if b == 0 and n in (-5, -4):
            found += [("in", 0, 4 + 2 * (n + 5)), ("in", 0, 5 + 2 * (n + 5))]
        if b > 0 and n == -5:
            found.append(("out", b - 1, TT - 1))
        if b < B and 27 <= n <= 33:
            found.append(("mid", b, n - 27))
    else:
        if n == 0:
            found.append(("mid", b, TT - 1))
        if b + 1 < B and 29 <= n <= 32:
            found.append(("in", b + 1, n - 29))
        if b + 1 < B and n in (33, 34):
            found += [("in", b + 1, 4 + 2 * (n - 33)), ("in", b + 1, 5 + 2 * (n - 33))]
        if 30 <= n <= 36:
            found.append(("out", b, n - 30))
    return found


def jobs_before(b, layer, n):
    if n is None:
        return []
    if layer == 0 and n == -5:
        found = jobs(b - 1, 1, 36) if b > 0 else []
    elif layer == 1 and n == 0:
        found = jobs(b, 0, 33)
    else:
        found = jobs(b, layer, n - 1)
    return [job for job in found if job[0] != "out"]


def turned(kind, b, t):
    return b * 2 * TT + (TT if kind == "mid" else 0) + t


def item_of(m):
    return m + 5 + max(0, (m + 1) // 4 + (1 if m >= -1 else 0))


def key_item_of(m):
    return item_of(m) + 1


def build(nc, x, wq, wk, wv, wo, wg, wu, wd, cos_t, sin_t, causal, eye, out):
    with ExitStack() as ctx:
        def sb(name, shape, dtype=F32):
            return ctx.enter_context(nc.sbuf_tensor(name, shape, dtype))

        def sem(name):
            return ctx.enter_context(nc.semaphore(name))

        Xh = sb("x_hi", [P, KT, S], F32R)
        Xl = sb("x_lo", [P, KT, S], F32R)
        Y = sb("y_acc", [P, TT, DM])
        Wh = sb("w_hi", [P, 8, W], F32R)
        Wl = sb("w_lo", [P, 8, W], F32R)
        Oh = sb("wout_hi", [P, 4, W], F32R)
        Ol = sb("wout_lo", [P, 4, W], F32R)
        stage = sb("stage", [P, RING_A, W])
        big_h = sb("big_hi", [P, 2, 4, W], F32R)
        big_l = sb("big_lo", [P, 2, 4, W], F32R)
        Kh = sb("k_hi", [P, W], F32R)
        Kl = sb("k_lo", [P, W], F32R)
        KTh = sb("kt_hi", [P, 4, P], F32R)
        KTl = sb("kt_lo", [P, 4, P], F32R)
        Vh = sb("v_hi", [P, 4, VP], F32R)
        Vl = sb("v_lo", [P, 4, P], F32R)
        Sh = sb("s_hi", [P, 4, P], F32R)
        Sl = sb("s_lo", [P, 4, P], F32R)
        Ah = sb("a_hi", [P, 4, P], F32R)
        Al = sb("a_lo", [P, 4, P], F32R)
        Sth = sb("st_hi", [P, 2, P], F32R)
        Stl = sb("st_lo", [P, 2, P], F32R)
        ones = sb("ones", [P, P], F32R)
        mask = sb("mask", [P, P])
        ident = sb("ident", [P, P])
        scr = sb("scratch", [P, 18, W])
        msk = sb("masks", [P, 6, W], BF16)
        xr = sb("x_rows", [P, 2, W])
        small = sb("small", [P, 64])
        mhalf, eps_den, eps_ln = [small[:, i:i + 1] for i in range(3)]
        stat, mv, rstd = {}, {}, {}
        for i, kind in enumerate(KINDS):
            at = 4 + 20 * i
            stat[kind] = small[:, at:at + 12].rearrange("p (k c) -> p k c", k=2)
            mv[kind] = small[:, at + 12:at + 16].rearrange("p (k c) -> p k c", k=2)
            rstd[kind] = small[:, at + 16:at + 18]

        rot, xq, Eq, fq, vT, xk, Ek, kf, Sf, r0, Tn, of = [scr[:, i, :] for i in range(12)]
        cosb = scr[:, 12:14, :]
        sinb = scr[:, 14:16, :]
        YF = scr[:, 0:8, :]
        hid = scr[:, 8:12, :]
        ab = scr[:, 12:16, :]
        sg = scr[:, 16, :]
        Wmax = [scr[:, 17, :], ab[:, 1, :]]
        c01, c23, pw, qw, rr, m2 = [msk[:, i, :] for i in range(6)]
        m0 = qw
        def xt_in(b, t):
            if b == 0:
                return scr[:, 4 + t, :]
            return xr[:, t % 2, :] if t < 4 else stage[:, t - 3, :]

        xn_mid = [scr[:, 0, :], scr[:, 17, :]]

        bank = [ctx.enter_context(nc.psum_tensor(f"bank{i}", [P, W], F32)) for i in range(8)]
        psS, psQ, psK, psO, psD, psY, psSt, psT = bank
        psG, psU, psYF = bank[0:2], [bank[3], bank[2]], bank[4:6]
        psX_in, psX_mid = [bank[6], bank[7]], [psK, psT]

        ident_ld = sem("ident_ld")
        mask_ld = sem("mask_ld")
        const_ok = sem("const_ok")
        tab_ld = sem("tab_ld")
        ld_a = [sem(f"ld_a{i}") for i in range(RING_A)]
        ld_f = [sem(f"ld_f{i}") for i in range(RING_F)]
        act_w = sem("act_w")
        pool_w = sem("pool_w")
        dve_w = sem("dve_w")
        act_wf = sem("act_wf")
        pool_wf = sem("pool_wf")
        ld_in = [sem(f"ld_in{t}") for t in range(TT)]
        ld_mid = [sem(f"ld_mid{i}") for i in range(2)]
        st_out = sem("st_out")
        dve_stat = {kind: sem(f"dve_stat_{kind}") for kind in KINDS}
        dve_var = {kind: sem(f"dve_var_{kind}") for kind in KINDS}
        pool_rs = {kind: sem(f"pool_rs_{kind}") for kind in KINDS}
        pool_eps = sem("pool_eps")
        dve_norm = {kind: sem(f"dve_norm_{kind}") for kind in KINDS[1:]}
        dve_xn = sem("dve_xn")
        pe_xt = sem("pe_xt")
        act_xh = sem("act_xh")
        dve_xl = sem("dve_xl")
        dve_res = sem("dve_res")
        dve_out = sem("dve_out")
        dve_self = sem("dve_self")
        dve_const = sem("dve_const")
        pe_q = sem("pe_q")
        pe_kv = sem("pe_kv")
        pe_tr = sem("pe_tr")
        pe_s = sem("pe_s")
        pe_pv = sem("pe_pv")
        pe_st = sem("pe_st")
        pe_y = sem("pe_y")
        act_rot = sem("act_rot")
        act_exp = sem("act_exp")
        act_fh = sem("act_fh")
        act_vt = sem("act_vt")
        act_kvh = sem("act_kvh")
        act_ln = sem("act_ln")
        act_r0 = sem("act_r0")
        act_sh = sem("act_sh")
        act_sth = sem("act_sth")
        act_ah = sem("act_ah")
        dve_t1 = sem("dve_t1")
        dve_t2 = sem("dve_t2")
        dve_x = sem("dve_x")
        dve_m = sem("dve_m")
        dve_f = sem("dve_f")
        dve_sf = sem("dve_sf")
        dve_T = sem("dve_T")
        dve_U = sem("dve_U")
        dve_a = sem("dve_a")
        dve_kvl = sem("dve_kvl")
        dve_stl = sem("dve_stl")
        y_ok = sem("y_ok")
        pool_fl = sem("pool_fl")
        pool_sl = sem("pool_sl")
        pool_al = sem("pool_al")
        pe_g = sem("pe_g")
        pe_u = sem("pe_u")
        pe_d = sem("pe_d")
        act_sg = sem("act_sg")
        act_ab = sem("act_ab")
        act_hh = sem("act_hh")
        dve_h = sem("dve_h")
        dve_rank = sem("dve_rank")
        dve_hs = sem("dve_hs")
        dve_hl = sem("dve_hl")
        yf_ok = sem("yf_ok")
        pool_hl = sem("pool_hl")

        block = ctx.enter_context(nc.Block())

        def need(eng, s, b, total, U, per_unit, k):
            if isinstance(U, int):
                k, U = k + U * per_unit, None
                if k <= 0:
                    return
                eng.wait_ge(s, b * total + k)
            else:
                assert k > 0
                eng.wait_ge(s, b * total + U * per_unit + k)

        w_of_piece_f = [0, 4, 1, 5, 2, 6, 3, 7]

        def q_tile(s, n):
            return psD if n in (-4, -2) else psQ

        def walk_a(eng, b, slot):
            for s in range(-5, 2):
                slot(b, 0, s, s)
            with eng.Fori(0, NU - 1) as U:
                for s in range(2, 2 + SPU):
                    slot(b, U, s, None)
            for s in range(2, 2 + SPU):
                slot(b, NU - 1, s, SPU * (NU - 1) + s)

        def walk_f(eng, b, slot):
            for s in range(0, 5):
                slot(b, 0, s, s)
            with eng.Fori(0, NU - 1) as U:
                for s in range(5, 5 + SPU):
                    slot(b, U, s, None)
            for s in range(5, 5 + SPU):
                slot(b, NU - 1, s, SPU * (NU - 1) + s)

        def exists(n, low, high):
            return n is None or low <= n <= high

        @block.sync
        def _(sp):
            def x_in(b, t):
                if b > 0:
                    if t >= 4:
                        sp.wait_ge(pool_wf, b * T_W_F)
                    elif t >= 2:
                        sp.wait_ge(pe_xt, turned("in", b, t - 2) + 1)
                    else:
                        sp.wait_ge(dve_res, b * TT)
                sp.dma_start(xt_in(b, t), x[b, t * P:(t + 1) * P, :]).then_inc(ld_in[t], 16)

            def x_mid(b, t):
                if t >= 2:
                    sp.wait_ge(dve_res, b * TT + t - 1)
                elif b > 0:
                    sp.wait_ge(pe_xt, turned("in", b, TT))
                sp.dma_start(xr[:, t % 2, :], x[b, t * P:(t + 1) * P, :]).then_inc(ld_mid[t % 2], 16)

            def tables(b):
                if b > 0:
                    sp.wait_ge(dve_hs, b * 8 * NU)
                sp.dma_start(cosb, cos_t.rearrange("p (a t) -> p a t", a=2)).then_inc(tab_ld, 16)
                sp.dma_start(sinb, sin_t.rearrange("p (a t) -> p a t", a=2)).then_inc(tab_ld, 16)

            def piece_a(b, U, i, src):
                before = i - RING_A
                r, u = before - A_PRO, U
                if i >= A_PRO and r < 0 and not (isinstance(U, int) and U == 0):
                    r, u = r + A_UNIT, U - 1
                if i < A_PRO or r < 0:
                    if before >= 0:
                        sp.wait_ge(pool_w, b * T_WPOOL_A + before + 1)
                elif r in W_DVE:
                    sp.wait_ge(dve_w, b * T_WDVE + 3 * u + W_DVE[r])
                else:
                    sp.wait_ge(pool_w, b * T_WPOOL_A + A_PRO + 7 * u + W_POOL[r])
                if b > 0 and 1 <= i <= 4:
                    sp.wait_ge(pe_xt, turned("in", b, 3 + i) + 1)
                sp.dma_start(stage[:, i % RING_A, :], src).then_inc(ld_a[i % RING_A], 16)

            def unit_a(b, U, last):
                for j in range(4):
                    piece_a(b, U, A_PRO + j, wo[U, j])
                if not last:
                    for i, src in enumerate([wq[U + 1, 0], wq[U + 1, 1], wq[U + 1, 2], wq[U + 1, 3],
                                             wk[U + 1], wv[U + 1]]):
                        piece_a(b, U, A_PRO + 4 + i, src)

            def piece_f(b, U, i, src):
                if i >= RING_F:
                    sp.wait_ge(pool_wf, b * T_W_F + F_UNIT * U + i - RING_F + 1)
                sp.dma_start(stage[:, i % RING_F, :], src).then_inc(ld_f[i % RING_F], 16)

            def piece_f0(b, i):
                piece_f(b, 0, i, (wg, wu)[i % 2][0, i // 2])

            def unit_f(b, U, last):
                for j in range(4):
                    piece_f(b, U, F_PRO + j, wd[U, j])
                if not last:
                    for j in range(4):
                        piece_f(b, U, F_PRO + 4 + 2 * j, wg[U + 1, j])
                        piece_f(b, U, F_PRO + 5 + 2 * j, wu[U + 1, j])

            def store(b, t):
                sp.wait_ge(dve_out, b * TT + t + 1)
                sp.dma_start(out[b, t * P:(t + 1) * P, :], Y[:, t, :]).then_inc(st_out, 16)

            first_a = [wq[0, 0], wq[0, 1], wq[0, 2], wq[0, 3], wk[0], wv[0]]
            for t in range(4):
                x_in(0, t)
                if t == 1:
                    sp.dma_start(ident[:, :], eye).then_inc(ident_ld, 16)
            for i in range(5):
                piece_a(0, 0, i, first_a[i])
                if i == 0:
                    sp.dma_start(mask[:, :], causal).then_inc(mask_ld, 16)
                if i < 4:
                    x_in(0, 4 + i)
            tables(0)
            piece_a(0, 0, 5, first_a[5])
            for b in range(B):
                unit_a(b, 0, False)
                with sp.Fori(1, NU - 1) as U:
                    unit_a(b, U, False)
                x_mid(b, 0)
                x_mid(b, 1)
                unit_a(b, NU - 1, True)
                sp.wait_ge(pool_w, (b + 1) * T_WPOOL_A)
                sp.wait_ge(dve_w, (b + 1) * T_WDVE)
                for i in range(4):
                    piece_f0(b, i)
                x_mid(b, 2)
                x_mid(b, 3)
                for i in range(4, 6):
                    piece_f0(b, i)
                x_mid(b, 4)
                for i in range(6, 8):
                    piece_f0(b, i)
                for t in range(5, TT):
                    x_mid(b, t)
                with sp.Fori(0, NU - 1) as U:
                    unit_f(b, U, False)
                if b + 1 == B:
                    unit_f(b, NU - 1, True)
                    for t in range(TT):
                        store(b, t)
                else:
                    x_in(b + 1, 0)
                    x_in(b + 1, 1)
                    unit_f(b, NU - 1, True)
                    sp.wait_ge(pool_wf, (b + 1) * T_W_F)
                    piece_a(b + 1, 0, 0, first_a[0])
                    x_in(b + 1, 2)
                    x_in(b + 1, 3)
                    for t in range(4, TT):
                        x_in(b + 1, t)
                    store(b, 0)
                    store(b, 1)
                    tables(b + 1)
                    store(b, 2)
                    store(b, 3)
                    piece_a(b + 1, 0, 1, first_a[1])
                    piece_a(b + 1, 0, 2, first_a[2])
                    store(b, 4)
                    for i in range(3, 6):
                        piece_a(b + 1, 0, i, first_a[i])
                    for t in range(5, TT):
                        store(b, t)
            sp.wait_ge(st_out, B * TT * 16)

        @block.tensor
        def _(pe):
            def three(ps, whi, wlo, xhi, xlo, first, last):
                pe.matmul(ps, whi, xhi, start=first, stop=False, skip_group_check=True)
                pe.matmul(ps, wlo, xhi, start=False, stop=False, skip_group_check=True)
                return pe.matmul(ps, whi, xlo, start=False, stop=last, skip_group_check=True)

            def turn(kind, b, t):
                k = turned(kind, b, t)
                ps, xn = (psX_in[t % 2], xt_in(b, t)) if kind == "in" else (psX_mid[t % 2], xn_mid[t % 2])
                pe.wait_ge(dve_xn, k + 1)
                if k > 1:
                    pe.wait_ge(dve_xl, k - 1)
                if kind == "mid" and t == 0:
                    pe.wait_ge(act_vt, (b + 1) * T_STEP)
                if kind == "mid" and t == 1:
                    pe.wait_ge(dve_kvl, (b + 1) * T_KV)
                for kk in range(KT):
                    ins = pe.transpose(ps[:, kk * P:(kk + 1) * P], xn[:, kk * P:(kk + 1) * P], ident[:, :])
                ins.then_inc(pe_xt, 1)

            def project(ps, w, step):
                for kk in range(KT):
                    ins = three(ps[:, :], Wh[:, w, kk * P:(kk + 1) * P], Wl[:, w, kk * P:(kk + 1) * P],
                                Xh[:, kk, step * W:(step + 1) * W], Xl[:, kk, step * W:(step + 1) * W],
                                kk == 0, kk == KT - 1)
                return ins

            def scores(b, U, s, n):
                if s % 4 == 0:
                    need(pe, pool_fl, b, T_ITEM, U, 10, 5 * (s // 4) + 5)
                need(pe, dve_sf, b, T_SLOT, U, SPU, s)
                par, c = (s // 4) % 2, s % 4
                t = slice(c * P, (c + 1) * P)
                ins = three(psS[:, :].rearrange("p (h t) -> p h t", h=4), Kh[:, t], Kl[:, t],
                            big_h[:, par, :, t], big_l[:, par, :, t], True, True)
                ins.then_inc(pe_s, 1)

            def slot_a(b, U, s, n):
                if exists(n, 29, 31) and n is not None:
                    scores(b, U, s, n)
                if exists(n, 1, 32):
                    m = s - 1
                    mu, ms = m // SPU, m % SPU
                    par, c = (m // 4) % 2, m % 4
                    t = slice(c * P, (c + 1) * P)
                    need(pe, pool_sl, b, T_SLOT, U, SPU, m + 1)
                    if c == 0:
                        need(pe, dve_kvl, b, T_KV, U, 4, 2 * (m // 4) + 1)
                    need(pe, dve_a, b, T_SLOT, U, SPU, m)
                    o3 = psO[:, :].rearrange("p (h t) -> p h t", h=4)
                    d3 = psD[:, :].rearrange("p (h t) -> p h t", h=4)
                    first = ms == 0
                    three(o3, Vh[:, c, 0:P], Vl[:, c, :], Sh[:, :, :], Sl[:, :, :], True, first)
                    pe.matmul(d3, ones[:, :], Sh[:, :, :], start=True, stop=False, skip_group_check=True)
                    ins = pe.matmul(d3, ones[:, :], Sl[:, :, :], start=False, stop=first, skip_group_check=True)
                    if not first:
                        need(pe, dve_stl, b, T_STATE, U, 7, 7 * mu + ms)
                        three(o3, Sth[:, 0, :], Stl[:, 0, :], big_h[:, par, :, t], big_l[:, par, :, t], False, True)
                        ins = three(d3, Sth[:, 1, :], Stl[:, 1, :], big_h[:, par, :, t], big_l[:, par, :, t],
                                    False, True)
                    ins.then_inc(pe_pv, 1)
                    if ms < SPU - 1:
                        if c == 0:
                            need(pe, dve_kvl, b, T_KV, U, 4, 2 * (m // 4) + 2)
                        if first:
                            need(pe, dve_stl, b, T_STATE, U, 7, 7 * mu)
                        pe.matmul(psSt[:, 0:VP], KTh[:, c, :], Vh[:, c, :], start=first, stop=False,
                                  skip_group_check=True)
                        pe.matmul(psSt[:, 0:VP], KTl[:, c, :], Vh[:, c, :], start=False, stop=False,
                                  skip_group_check=True)
                        pe.matmul(psSt[:, 0:P], KTh[:, c, :], Vl[:, c, :], start=False, stop=True,
                                  skip_group_check=True).then_inc(pe_st, 1)
                if s % 4 == 0 and exists(n, 0, 28):
                    need(pe, act_vt, b, T_STEP, U, 2, s // 4 + 1)
                    need(pe, dve_kvl, b, T_KV, U, 4, 2 * (s // 4))
                    for c in range(4):
                        ins = pe.transpose(psT[:, c * P:(c + 1) * P], vT[:, c * P:(c + 1) * P], ident[:, :])
                    ins.then_inc(pe_tr, 1)
                if n == -5:
                    pe.wait_ge(dve_xl, turned("in", b, 4))
                    if b > 0:
                        pe.wait_ge(act_sg, b * T_SLOT)
                        pe.wait_ge(dve_h, b * T_SLOT)
                if n == -1:
                    pe.wait_ge(dve_xl, turned("in", b, TT))
                if n == 0 and b > 0:
                    pe.wait_ge(yf_ok, b * (T_SLOT + 2))
                if exists(n, 0, 28):
                    scores(b, U, s, n)
                for kind, jb, t in jobs_before(b, 0, n):
                    turn(kind, jb, t)
                if exists(n, 2, 33):
                    need(pe, pool_al, b, T_SLOT, U, SPU, s - 1)
                    need(pe, y_ok, b, T_SLOT + 1, U, SPU, s - 1)
                    for h in range(4):
                        if s == 2:
                            if h < 2:
                                need(pe, dve_w, b, T_WDVE, U, 3, W_DVE[h])
                            else:
                                need(pe, pool_w, b, T_WPOOL_A, U, 7, A_PRO + W_POOL[h])
                        ins = three(psY[:, :], Ah[:, h, :], Al[:, h, :], Oh[:, h, :], Ol[:, h, :], h == 0, h == 3)
                    ins.then_inc(pe_y, 1)
                if s % 4 == 0 and exists(n, 0, 28):
                    need(pe, dve_kvl, b, T_KV, U, 4, 2 * (s // 4) + 1)
                    for c in range(4):
                        ins = pe.transpose(psT[:, c * P:(c + 1) * P], kf[:, c * P:(c + 1) * P], ident[:, :])
                    ins.then_inc(pe_tr, 1)
                if exists(n, -5, 26):
                    j = (s + 1) % 4
                    if n is not None and n < -1:
                        pe.wait_ge(pool_w, b * T_WPOOL_A + j + 1)
                    elif s == 3:
                        need(pe, dve_w, b, T_WDVE, U, 3, W_DVE[4])
                    elif 4 <= s <= 6:
                        need(pe, pool_w, b, T_WPOOL_A, U, 7, A_PRO + W_POOL[s + 1])
                    if n is None or n >= -1:
                        need(pe, dve_t1, b, T_ITEM, U, 10, item_of(s - 1) + 1 if s > -1 else item_of(-3) + 1)
                    elif n >= -3:
                        need(pe, dve_t1, b, T_ITEM, U, 10, item_of(s - 2) + 1)
                    elif n == -4 and b > 0:
                        pe.wait_ge(yf_ok, b * (T_SLOT + 2))
                    project(q_tile(s, n), j, ((s + 1) // 4 + 1) % 2).then_inc(pe_q, 1)
                if s % 4 == 2 and exists(n, -2, 26):
                    if n is not None and n < 0:
                        pe.wait_ge(pool_w, b * T_WPOOL_A + 5)
                    elif s == 6:
                        need(pe, pool_w, b, T_WPOOL_A, U, 7, A_PRO + W_POOL[8])
                    need(pe, act_vt, b, T_STEP, U, 2, (s + 2) // 4)
                    project(psK, 4, ((s + 2) // 4) % 2).then_inc(pe_kv, 1)
                if s % 4 == 3 and exists(n, -1, 27):
                    if n is not None and n < 0:
                        pe.wait_ge(pool_w, b * T_WPOOL_A + 6)
                    elif s == 7:
                        need(pe, pool_w, b, T_WPOOL_A, U, 7, A_PRO + W_POOL[9])
                    need(pe, dve_t1, b, T_ITEM, U, 10, key_item_of(s - 1) + 1)
                    project(psK, 5, ((s + 1) // 4) % 2).then_inc(pe_kv, 1)

            def slot_f(b, U, s, n):
                j = s % 4
                if n == 0:
                    pe.wait_ge(dve_xl, turned("mid", b, 4))
                    pe.wait_ge(dve_sf, (b + 1) * T_SLOT)
                    pe.wait_ge(dve_t1, (b + 1) * T_ITEM)
                    pe.wait_ge(dve_a, (b + 1) * T_SLOT)
                if n == 1:
                    pe.wait_ge(dve_xl, turned("mid", b, TT - 1))
                if n == 4:
                    pe.wait_ge(dve_xl, turned("mid", b, TT))
                if n == 5:
                    pe.wait_ge(y_ok, (b + 1) * (T_SLOT + 1))
                if exists(n, 0, 31):
                    if n is not None and n < 4:
                        pe.wait_ge(pool_wf, b * T_W_F + 2 * j + 2)
                    elif s >= 8 and s < 12:
                        need(pe, pool_wf, b, T_W_F, U, F_UNIT, F_PRO + 4 + 2 * j + 2)
                    need(pe, act_sg, b, T_SLOT, U, SPU, s - 1)
                    project(psG[s % 2], j, (s // 4) % 2).then_inc(pe_g, 1)
                    need(pe, dve_h, b, T_SLOT, U, SPU, s - 1)
                    project(psU[s % 2], 4 + j, (s // 4) % 2).then_inc(pe_u, 1)
                for kind, jb, t in jobs_before(b, 1, n):
                    turn(kind, jb, t)
                if exists(n, 5, 36):
                    y = s - 5
                    d, ts = y // 4, y % 4
                    need(pe, yf_ok, b, T_SLOT + 2, U, SPU, y + 1)
                    for i in range(4):
                        if ts == 0 and i < 2:
                            need(pe, pool_hl, b, 4 * NU, U, 4, 2 * d + i + 1)
                        elif ts == 0:
                            need(pe, dve_hl, b, 4 * NU, U, 4, 2 * d + i - 1)
                        if s == 5:
                            need(pe, pool_wf, b, T_W_F, U, F_UNIT, F_PRO + i + 1)
                        ins = three(psYF[y % 2][:, :], big_h[:, d % 2, i, ts * P:(ts + 1) * P],
                                    big_l[:, d % 2, i, ts * P:(ts + 1) * P], Oh[:, i, :], Ol[:, i, :],
                                    i == 0, i == 3)
                    ins.then_inc(pe_d, 1)

            pe.wait_ge(const_ok, 1)
            pe.wait_ge(ident_ld, 16)
            for t in range(4):
                turn("in", 0, t)
            for b in range(B):
                walk_a(pe, b, slot_a)
                walk_f(pe, b, slot_f)

        @block.scalar
        def _(act):
            copy = nc.scalar.copy

            def split_x(kind, b, t):
                ps = (psX_in if kind == "in" else psX_mid)[t % 2]
                act.wait_ge(pe_xt, turned(kind, b, t) + 1)
                copy(Xh[:, :, t * P:(t + 1) * P], ps[:, :].rearrange("p (c t) -> p c t", c=KT)).then_inc(act_xh, 1)

            def raw(b, ring, lds, i, U, per_unit, total):
                slot_ = i % ring
                k = i // ring + 1
                act.wait_ge(lds[slot_], (b * total + U * (per_unit // ring) + k) * 16)
                return stage[:, slot_, :]

            def count_a(slot_):
                return sum(1 for i in range(T_WACT_A) if i % RING_A == slot_)

            def count_f(slot_):
                return sum(1 for i in range(T_W_F) if i % RING_F == slot_)

            def wsplit_a(b, U, i, dst):
                copy(dst, raw(b, RING_A, ld_a, i, U, A_UNIT, count_a(i % RING_A))).then_inc(act_w, 1)

            def wsplit_f(b, U, i, dst):
                copy(dst, raw(b, RING_F, ld_f, i, U, F_UNIT, count_f(i % RING_F))).then_inc(act_wf, 1)

            def turn_half(src):
                def to(dst):
                    copy(dst[HALF:P, :], src[0:HALF, :])
                    return copy(dst[0:HALF, :], src[HALF:P, :])
                return to

            def slot_a(b, U, s, n):
                if n is not None and n < 0:
                    wsplit_a(b, 0, n + 6, Wh[:, n + 6, :])
                m = s - 1
                mu, ms = m // SPU, m % SPU
                it = item_of(m)
                q_item = exists(n, -4, 27)
                k_item = m % 4 == 2 and exists(n, -1, 27)
                if n == -5:
                    nc.scalar.preload_act_table_set("natural_log_exp_and_others")
                if n == -4 and b > 0:
                    act.wait_ge(dve_out, b * TT)
                if q_item:
                    need(act, pe_q, b, T_SLOT, U, SPU, m + 6)
                    need(act, dve_x, b, T_ITEM, U, 10, it)
                    turn_half(q_tile(m, n - 1 if n is not None else None))(rot).then_inc(act_rot, 1)
                if k_item:
                    need(act, pe_kv, b, T_KV, U, 4, 2 * ((s + 1) // 4) + 1)
                    need(act, pe_tr, b, T_KV, U, 4, 2 * ((s + 1) // 4))
                    turn_half(psK)(vT).then_inc(act_rot, 1)
                if exists(n, 1, 32) and ms < SPU - 1:
                    need(act, pe_st, b, T_STATE, U, 7, 7 * mu + ms + 1)
                    copy(Sth[:, 0, :], psSt[:, 0:P])
                    copy(Sth[:, 1, :], psSt[:, P:P + 1].to_broadcast([P, P])).then_inc(act_sth, 1)
                if exists(n, 1, 32):
                    need(act, pe_pv, b, T_SLOT, U, SPU, s)
                    need(act, dve_U, b, T_SLOT, U, SPU, s - 1)
                    nc.scalar.activation(r0, psD[:, :], ACT.Ln, bias=eps_den[:, 0:1]).then_inc(act_ln, 1)
                if q_item:
                    need(act, dve_x, b, T_ITEM, U, 10, it + 1)
                    nc.scalar.activation(Eq, xq, ACT.Exp).then_inc(act_exp, 1)
                if s % 4 == 0 and exists(n, 0, 28):
                    need(act, pe_tr, b, T_KV, U, 4, 2 * (s // 4) + 1)
                    copy(Vh[:, :, 0:P], psT[:, :].rearrange("p (c d) -> p c d", c=4)).then_inc(act_kvh, 1)
                if exists(n, 1, 32):
                    need(act, act_ln, b, T_SLOT, U, SPU, s)
                    nc.scalar.activation(r0, r0, ACT.Exp, scale=-1.0).then_inc(act_r0, 1)
                if k_item:
                    need(act, dve_x, b, T_ITEM, U, 10, it + 2)
                    nc.scalar.activation(Ek, xk, ACT.Exp).then_inc(act_exp, 1)
                if exists(n, 0, 31):
                    need(act, dve_sf, b, T_SLOT, U, SPU, s + 1)
                    need(act, pe_pv, b, T_SLOT, U, SPU, s)
                    copy(Sh[:, :, :].rearrange("p h t -> p (h t)"), Sf).then_inc(act_sh, 1)
                for job in jobs_before(b, 0, n):
                    split_x(*job)
                if q_item:
                    need(act, dve_f, b, T_ITEM, U, 10, it + 1)
                    if m >= 3 or n is None:
                        need(act, pe_pv, b, T_SLOT, U, SPU, s)
                    copy(big_h[:, ((m + 1) // 4 + 1) % 2, (m + 1) % 4, :], fq).then_inc(act_fh, 1)
                if k_item:
                    need(act, dve_f, b, T_ITEM, U, 10, it + 2)
                    if m >= 2:
                        need(act, pe_s, b, T_SLOT, U, SPU, s + 1)
                    copy(Kh[:, :], kf).then_inc(act_fh, 1)
                if exists(n, 1, 32):
                    need(act, dve_a, b, T_SLOT, U, SPU, s)
                    need(act, pe_y, b, T_SLOT, U, SPU, s - 1)
                    copy(Ah[:, :, :].rearrange("p h t -> p (h t)"), of).then_inc(act_ah, 1)
                if s == 2 and exists(n, 2, 25):
                    need(act, pe_q, b, T_SLOT, U, SPU, 5)
                    wsplit_a(b, U, A_PRO + 4, Wh[:, 0, :])
                if s == 3 and exists(n, 2, 25):
                    need(act, pe_q, b, T_SLOT, U, SPU, 7)
                    wsplit_a(b, U, A_PRO + 5, Wh[:, 1, :])
                    wsplit_a(b, U, A_PRO + 6, Wh[:, 2, :])
                if s == 4 and exists(n, 2, 25):
                    need(act, pe_q, b, T_SLOT, U, SPU, 8)
                    wsplit_a(b, U, A_PRO + 7, Wh[:, 3, :])
                    need(act, pe_kv, b, T_KV, U, 4, 3)
                    wsplit_a(b, U, A_PRO + 8, Wh[:, 4, :])
                if s == 5 and exists(n, 2, 25):
                    need(act, pe_kv, b, T_KV, U, 4, 4)
                    wsplit_a(b, U, A_PRO + 9, Wh[:, 5, :])
                if s == 9 and exists(n, 2, 25):
                    need(act, pe_y, b, T_SLOT, U, SPU, s - 1)
                    for h in range(4):
                        wsplit_a(b, U + 1, A_PRO + h, Oh[:, h, :])
                if n == 1:
                    for h in range(4):
                        wsplit_a(b, 0, A_PRO + h, Oh[:, h, :])
                if s % 4 == 3 and exists(n, -1, 27):
                    need(act, pe_kv, b, T_KV, U, 4, 2 * ((s + 1) // 4) + 2)
                    need(act, dve_x, b, T_ITEM, U, 10, it + 2)
                    copy(vT, psK[:, :]).then_inc(act_vt, 1)
                if s % 4 == 0 and exists(n, 0, 28):
                    need(act, pe_tr, b, T_KV, U, 4, 2 * (s // 4) + 2)
                    copy(KTh[:, :, :].rearrange("p c d -> p (c d)"), psT[:, :]).then_inc(act_kvh, 1)
                if n is not None and 28 <= n <= 31:
                    act.wait_ge(pe_kv, (b + 1) * T_KV)
                    for i in (2 * (n - 28), 2 * (n - 28) + 1):
                        wsplit_f(b, 0, i, Wh[:, w_of_piece_f[i], :])

            def slot_f(b, U, s, n):
                j = s % 4
                if s == 5 and exists(n, 5, 29):
                    need(act, pe_g, b, T_SLOT, U, SPU, s + 1)
                    for i in range(4):
                        wsplit_f(b, U, F_PRO + i, Oh[:, i, :])
                if 5 <= s <= 8 and exists(n, 5, 28):
                    i = s - 5
                    need(act, pe_u, b, T_SLOT, U, SPU, s)
                    wsplit_f(b, U, F_PRO + 4 + 2 * i, Wh[:, i, :])
                    wsplit_f(b, U, F_PRO + 5 + 2 * i, Wh[:, 4 + i, :])
                if exists(n, 1, 32):
                    i = (s - 1) % 4
                    need(act, dve_h, b, T_SLOT, U, SPU, s)
                    need(act, dve_rank, b, T_STEP, U, 2, (s - 1) // 4)
                    nc.scalar.activation(ab[:, i, :], hid[:, i, :], ACT.Abs).then_inc(act_ab, 1)
                if exists(n, 0, 31):
                    need(act, pe_g, b, T_SLOT, U, SPU, s + 1)
                    need(act, dve_h, b, T_SLOT, U, SPU, s)
                    nc.scalar.activation(sg, psG[s % 2][:, :], ACT.Silu).then_inc(act_sg, 1)
                for job in jobs_before(b, 1, n):
                    split_x(*job)
                if j == 0 and exists(n, 4, 32):
                    d = s // 4 - 1
                    for i in range(4):
                        need(act, dve_hs, b, 8 * NU, U, 8, 4 * d + i + 1)
                        copy(big_h[:, d % 2, i, :], hid[:, i, :]).then_inc(act_hh, 1)
                if b + 1 < B and n == 33:
                    act.wait_ge(pe_u, (b + 1) * T_SLOT)
                    wsplit_a(b + 1, 0, 0, Wh[:, 0, :])

            act.wait_ge(const_ok, 1)
            wsplit_a(0, 0, 0, Wh[:, 0, :])
            for t in range(4):
                split_x("in", 0, t)
            for b in range(B):
                walk_a(act, b, slot_a)
                walk_f(act, b, slot_f)

        @block.vector
        def _(dve):
            def source(kind, b, t):
                return {"in": xt_in(b, t), "mid": Y[:, t, :], "out": YF[:, t, :]}[kind]

            def count(kind, b, t, second=False):
                return (b * TT + t) * (2 if kind == "mid" else 1) + second

            def variances(todo, second=False):
                for kind, b, t in todo:
                    if kind == "in":
                        dve.wait_ge(ld_in[t], (b + 1) * 16)
                    elif kind == "out":
                        dve.wait_ge(yf_ok, b * (T_SLOT + 2) + 2 + 24 + t + 1)
                    elif second:
                        dve.wait_ge(dve_res, b * TT + t + 1)
                    else:
                        dve.wait_ge(y_ok, b * (T_SLOT + 1) + 1 + 24 + t + 1)
                    dve.bn_stats(stat[kind][:, t % 2, :], source(kind, b, t)).then_inc(dve_stat[kind], 1)
                for kind, b, t in todo:
                    dve.wait_ge(dve_stat[kind], count(kind, b, t, second) + 1)
                    dve.bn_aggr(mv[kind][:, t % 2, :], stat[kind][:, t % 2, :]).then_inc(dve_var[kind], 1)

            def normalise(kind, b, t, dst, second=False):
                k = count(kind, b, t, second)
                dve.wait_ge(pool_rs[kind], k + 1)
                dve.wait_ge(dve_var[kind], k + 1)
                return dve.tensor_scalar(dst, source(kind, b, t), mv[kind][:, t % 2, 0:1],
                                         rstd[kind][:, t % 2:t % 2 + 1], ALU.subtract, ALU.mult)

            def middle(todo):
                todo = [job for job in todo if job[0] != "in"]
                for kind, b, t in todo:
                    normalise(kind, b, t, source(kind, b, t)).then_inc(dve_norm[kind], 1)
                for kind, b, t in todo:
                    if kind == "mid":
                        dve.wait_ge(dve_norm[kind], b * TT + t + 1)
                        dve.wait_ge(ld_mid[t % 2], (b * TT + t) // 2 * 16 + 16)
                        dve.tensor_tensor(Y[:, t, :], Y[:, t, :], xr[:, t % 2, :], ALU.add).then_inc(dve_res, 1)
                variances([job for job in todo if job[0] == "mid"], second=True)

            def late(todo):
                for kind, b, t in todo:
                    if kind == "out":
                        dve.wait_ge(dve_norm[kind], b * TT + t + 1)
                        dve.tensor_tensor(Y[:, t, :], YF[:, t, :], Y[:, t, :], ALU.add).then_inc(dve_out, 1)
                    else:
                        xn = xt_in(b, t) if kind == "in" else xn_mid[t % 2]
                        normalise(kind, b, t, xn, second=kind == "mid").then_inc(dve_xn, 1)

            def split_x(kind, b, t):
                ps = (psX_in if kind == "in" else psX_mid)[t % 2]
                dve.wait_ge(act_xh, turned(kind, b, t) + 1)
                dve.tensor_tensor(Xl[:, :, t * P:(t + 1) * P], ps[:, :].rearrange("p (c t) -> p c t", c=KT),
                                  Xh[:, :, t * P:(t + 1) * P].bitcast(F32), ALU.subtract).then_inc(dve_xl, 1)

            def wlo_a(b, U, r, dst, hi):
                need(dve, act_w, b, T_WACT_A, U, A_UNIT, A_PRO + r + 1)
                dve.tensor_tensor(dst, stage[:, (A_PRO + r) % RING_A, :], hi.bitcast(F32),
                                  ALU.subtract).then_inc(dve_w, 1)

            def slot_a(b, U, s, n):
                m = s - 1
                it = item_of(m)
                mu, ms = m // SPU, m % SPU
                q_item = exists(n, -4, 27)
                k_item = m % 4 == 2 and exists(n, -1, 27)
                pstep = ((m + 1) // 4 + 1) % 2
                todo = jobs(b, 0, n)
                variances(todo)
                if n == -4:
                    dve.wait_ge(tab_ld, b * 32 + 32)
                if q_item:
                    need(dve, act_rot, b, T_ITEM, U, 10, it + 1)
                    dve.tensor_tensor(xq, q_tile(m, n - 1 if n is not None else None)[:, :], cosb[:, pstep, :], ALU.mult).then_inc(dve_t1, 1)
                    dve.tensor_tensor(rot, rot, sinb[:, pstep, :], ALU.mult).then_inc(dve_t2, 1)
                if k_item:
                    kstep = ((s + 1) // 4) % 2
                    need(dve, act_rot, b, T_ITEM, U, 10, it + 2)
                    dve.tensor_tensor(xk, psK[:, :], cosb[:, kstep, :], ALU.mult).then_inc(dve_t1, 1)
                    dve.tensor_tensor(vT, vT, sinb[:, kstep, :], ALU.mult).then_inc(dve_t2, 1)
                if q_item:
                    need(dve, dve_t2, b, T_ITEM, U, 10, it + 1)
                    dve.tensor_tensor(xq, xq, rot, ALU.add).then_inc(dve_x, 1)
                if k_item:
                    need(dve, dve_t2, b, T_ITEM, U, 10, it + 2)
                    dve.tensor_tensor(xk, xk, vT, ALU.add).then_inc(dve_x, 1)
                if n == 0:
                    dve.wait_ge(mask_ld, 16)
                if exists(n, 0, 31):
                    need(dve, pe_s, b, T_SLOT, U, SPU, s + 1)
                    need(dve, pool_sl, b, T_SLOT, U, SPU, s)
                    dve.tensor_tensor(Sf.rearrange("p (h t) -> p h t", h=4),
                                      psS[:, :].rearrange("p (h t) -> p h t", h=4),
                                      mask[:, :].rearrange("p (o t) -> p o t", o=1).to_broadcast([P, 4, P]),
                                      ALU.mult).then_inc(dve_sf, 1)
                if exists(n, 1, 32) and ms < SPU - 1:
                    need(dve, act_sth, b, T_STATE, U, 7, 7 * mu + ms + 1)
                    dve.tensor_tensor(Stl[:, 0, :], psSt[:, 0:P], Sth[:, 0, :].bitcast(F32), ALU.subtract)
                    dve.tensor_tensor(Stl[:, 1, :], psSt[:, P:P + 1].to_broadcast([P, P]),
                                      Sth[:, 1, :].bitcast(F32), ALU.subtract).then_inc(dve_stl, 1)
                if s % 4 == 0 and exists(n, 0, 28):
                    need(dve, act_kvh, b, T_KV, U, 4, 2 * (s // 4) + 1)
                    dve.tensor_tensor(Vl[:, :, :], psT[:, :].rearrange("p (c d) -> p c d", c=4),
                                      Vh[:, :, 0:P].bitcast(F32), ALU.subtract).then_inc(dve_kvl, 1)
                if exists(n, 1, 32):
                    need(dve, act_r0, b, T_SLOT, U, SPU, s)
                    dve.scalar_tensor_tensor(Tn, psD[:, :], EPS_DEN, r0, ALU.add, ALU.mult).then_inc(dve_T, 1)
                if q_item:
                    need(dve, act_exp, b, T_ITEM, U, 10, it + 1)
                    dve.tensor_scalar(Eq, Eq, 1.0, None, ALU.min).then_inc(dve_m, 1)
                if exists(n, 1, 32):
                    need(dve, dve_T, b, T_SLOT, U, SPU, s)
                    dve.scalar_tensor_tensor(Tn, Tn, 2.0, r0, ALU.subtract, ALU.mult).then_inc(dve_U, 1)
                middle(todo)
                if q_item:
                    need(dve, dve_m, b, T_ITEM, U, 10, it + 1)
                    need(dve, pool_fl, b, T_ITEM, U, 10, it)
                    dve.scalar_tensor_tensor(fq, xq, 0.0, Eq, ALU.max, ALU.add).then_inc(dve_f, 1)
                if k_item:
                    need(dve, act_exp, b, T_ITEM, U, 10, it + 2)
                    dve.tensor_scalar(Ek, Ek, 1.0, None, ALU.min).then_inc(dve_m, 1)
                if exists(n, 1, 32):
                    need(dve, dve_U, b, T_SLOT, U, SPU, s)
                    need(dve, pool_al, b, T_SLOT, U, SPU, m)
                    dve.scalar_tensor_tensor(of, Tn, -1.0, psO[:, :], ALU.mult, ALU.mult).then_inc(dve_a, 1)
                if k_item:
                    need(dve, dve_m, b, T_ITEM, U, 10, it + 2)
                    dve.scalar_tensor_tensor(kf, xk, 0.0, Ek, ALU.max, ALU.add).then_inc(dve_f, 1)
                for job in jobs_before(b, 0, n):
                    split_x(*job)
                late(todo)
                if s == 2 and exists(n, 2, 25):
                    wlo_a(b, U, 4, Wl[:, 0, :], Wh[:, 0, :])
                if n == 2:
                    dve.wait_ge(y_ok, b * (T_SLOT + 1) + 1)
                if exists(n, 2, 33):
                    need(dve, pe_y, b, T_SLOT, U, SPU, s - 1)
                    t = (s - 2) % SPU
                    dve.tensor_tensor(Y[:, t, :], psY[:, :], Y[:, t, :], ALU.add).then_inc(y_ok, 1)
                if s == 9 and exists(n, 2, 25):
                    for h in range(2):
                        wlo_a(b, U + 1, h, Ol[:, h, :], Oh[:, h, :])
                if n == 1:
                    for h in range(2):
                        wlo_a(b, 0, h, Ol[:, h, :], Oh[:, h, :])
                if s % 4 == 0 and exists(n, 0, 28):
                    need(dve, act_kvh, b, T_KV, U, 4, 2 * (s // 4) + 2)
                    dve.tensor_tensor(KTl[:, :, :].rearrange("p c d -> p (c d)"), psT[:, :],
                                      KTh[:, :, :].rearrange("p c d -> p (c d)").bitcast(F32), ALU.subtract).then_inc(dve_kvl, 1)

            def slot_f(b, U, s, n):
                if exists(n, 1, 32):
                    i = (s - 1) % 4
                    need(dve, pe_u, b, T_SLOT, U, SPU, s)
                    need(dve, act_sg, b, T_SLOT, U, SPU, s)
                    if s >= 5:
                        d = (s - 1) // 4 - 1
                        if i < 2:
                            need(dve, pool_hl, b, 4 * NU, U, 4, 2 * d + i + 1)
                        else:
                            need(dve, dve_hl, b, 4 * NU, U, 4, 2 * d + i - 1)
                    dve.tensor_tensor(hid[:, i, :], psU[(s - 1) % 2][:, :], sg, ALU.mult).then_inc(dve_h, 1)
                todo = jobs(b, 1, n)
                variances(todo)

                def pair(i, c, steps):
                    need(dve, act_ab, b, T_SLOT, U, SPU, steps)
                    dve.tensor_tensor(c, ab[:, 2 * i, :], ab[:, 2 * i + 1, :], ALU.is_ge)
                    dve.tensor_tensor(Wmax[i], ab[:, 2 * i, :], ab[:, 2 * i + 1, :], ALU.max)
                    return dve.tensor_tensor(ab[:, 2 * i, :], ab[:, 2 * i, :], ab[:, 2 * i + 1, :], ALU.min)

                if s % 4 == 3 and exists(n, 3, 31):
                    pair(0, c01, s - 1).then_inc(dve_self, 1)
                if s % 4 == 0 and exists(n, 4, 32):
                    d = s // 4 - 1
                    pair(1, c23, s).then_inc(dve_self, 1)
                    k0, per = d * SELF_F, 2 * SELF_F

                    def own(k):
                        need(dve, dve_self, b, SELF, U, per, k0 + k)

                    own(2)
                    dve.tensor_tensor(pw, ab[:, 0, :], Wmax[1], ALU.is_ge).then_inc(dve_self, 1)
                    dve.tensor_tensor(qw, ab[:, 2, :], Wmax[0], ALU.is_gt).then_inc(dve_rank, 1)
                    own(3)
                    need(dve, dve_rank, b, T_STEP, U, 2, d + 1)
                    dve.tensor_tensor(rr, qw, pw, ALU.subtract).then_inc(dve_self, 1)
                    dve.tensor_tensor(pw, pw, qw, ALU.subtract).then_inc(dve_self, 1)
                    own(5)
                    dve.tensor_tensor(m0, c01, rr, ALU.is_gt).then_inc(dve_self, 1)
                    dve.tensor_tensor(m2, c23, pw, ALU.is_gt).then_inc(dve_self, 1)
                    dve.tensor_scalar(rr, rr, -1.0, 1.0, ALU.mult, ALU.add).then_inc(dve_self, 1)
                    dve.tensor_scalar(pw, pw, -1.0, 1.0, ALU.mult, ALU.add).then_inc(dve_self, 1)
                    own(6)
                    dve.tensor_tensor(hid[:, 0, :], hid[:, 0, :], m0, ALU.mult).then_inc(dve_hs, 1)
                    own(8)
                    dve.tensor_tensor(c01, c01, rr, ALU.is_lt).then_inc(dve_self, 1)
                    own(9)
                    dve.tensor_tensor(c23, c23, pw, ALU.is_lt).then_inc(dve_self, 1)
                    own(10)
                    dve.tensor_tensor(hid[:, 1, :], hid[:, 1, :], c01, ALU.mult).then_inc(dve_hs, 1)
                    own(7)
                    dve.tensor_tensor(hid[:, 2, :], hid[:, 2, :], m2, ALU.mult).then_inc(dve_hs, 1)
                    own(11)
                    dve.tensor_tensor(hid[:, 3, :], hid[:, 3, :], c23, ALU.mult).then_inc(dve_hs, 1)
                    for i in range(2, 4):
                        need(dve, act_hh, b, 8 * NU, U, 8, 4 * d + i + 1)
                        dve.tensor_tensor(big_l[:, d % 2, i, :], hid[:, i, :], big_h[:, d % 2, i, :].bitcast(F32),
                                          ALU.subtract).then_inc(dve_hl, 1)
                middle(todo)
                for job in jobs_before(b, 1, n):
                    split_x(*job)
                late(todo)
                if n == 5:
                    dve.wait_ge(yf_ok, b * (T_SLOT + 2) + 2)
                if exists(n, 5, 36):
                    y = s - 5
                    need(dve, pe_d, b, T_SLOT, U, SPU, y + 1)
                    t = y % TT
                    dve.tensor_tensor(YF[:, t, :], psYF[y % 2][:, :], YF[:, t, :], ALU.add).then_inc(yf_ok, 1)

            SELF_F = 11
            SELF = SELF_F * T_STEP

            dve.memset(eps_den[:, :], EPS_DEN)
            dve.memset(mhalf[:, :], -0.5)
            dve.memset(eps_ln[:, :], EPS_LN)
            dve.memset(rot, 1.0).then_inc(dve_const, 1)
            dve.memset(xq, 0.0).then_inc(dve_const, 1)
            dve.wait_ge(dve_const, 2)
            dve.tensor_copy(ones[:, :], rot[:, 0:P])
            dve.tensor_copy(Vh[:, :, P:P + 1], rot[:, 0:4].rearrange("p (c o) -> p c o", o=1))
            dve.tensor_copy(Vh[:, :, P + 1:P + 2], xq[:, 0:4].rearrange("p (c o) -> p c o", o=1)).then_inc(const_ok, 1)
            first = [("in", 0, t) for t in range(4)]
            variances(first[0:2])
            late(first[0:2])
            variances(first[2:4])
            for t in range(4):
                split_x("in", 0, t)
                if t < 2:
                    late(first[t + 2:t + 3])
            for b in range(B):
                walk_a(dve, b, slot_a)
                walk_f(dve, b, slot_f)
            todo = jobs(B, 0, -5)
            variances(todo)
            middle(todo)
            late(todo)

        @block.gpsimd
        def _(pool):
            eps_done = []

            def lo(dst, full, hi):
                return pool.tensor_tensor(dst, full, hi.bitcast(F32), ALU.subtract)

            def deviations(todo, second=False):
                for kind, b, t in todo:
                    k = (b * TT + t) * (2 if kind == "mid" else 1) + second
                    r = rstd[kind][:, t % 2:t % 2 + 1]
                    pool.wait_ge(dve_var[kind], k + 1)
                    pool.tensor_tensor(r, mv[kind][:, t % 2, 1:2], eps_ln[:, :], ALU.add).then_inc(pool_eps, 1)
                    eps_done.append(1)
                    pool.wait_ge(pool_eps, len(eps_done))
                    pool.tensor_tensor(r, r, mhalf[:, :], ALU.pow).then_inc(pool_rs[kind], 1)

            def wlo_a(b, U, i, dst, hi):
                need(pool, act_w, b, T_WACT_A, U, A_UNIT, i + 1)
                lo(dst, stage[:, i % RING_A, :], hi).then_inc(pool_w, 1)

            def wlo_f(b, U, i, dst, hi):
                need(pool, act_wf, b, T_W_F, U, F_UNIT, i + 1)
                lo(dst, stage[:, i % RING_F, :], hi).then_inc(pool_wf, 1)

            def slot_a(b, U, s, n):
                m = s - 1
                it = item_of(m)
                deviations(jobs(b, 0, n))
                deviations([job for job in jobs(b, 0, n) if job[0] == "mid"], second=True)
                if n is not None and n < 0:
                    wlo_a(b, 0, n + 6, Wl[:, n + 6, :], Wh[:, n + 6, :])
                if n == -1:
                    if b > 0:
                        pool.wait_ge(st_out, b * TT * 16)
                    pool.memset(Y[:, :, :], 0.0).then_inc(y_ok, 1)
                if exists(n, 0, 31):
                    need(pool, act_sh, b, T_SLOT, U, SPU, s + 1)
                    lo(Sl[:, :, :].rearrange("p h t -> p (h t)"), Sf,
                       Sh[:, :, :].rearrange("p h t -> p (h t)")).then_inc(pool_sl, 1)
                if exists(n, -4, 27):
                    par, h = ((m + 1) // 4 + 1) % 2, (m + 1) % 4
                    need(pool, act_fh, b, T_ITEM, U, 10, it + 1)
                    lo(big_l[:, par, h, :], fq, big_h[:, par, h, :]).then_inc(pool_fl, 1)
                if m % 4 == 2 and exists(n, -1, 27):
                    need(pool, act_fh, b, T_ITEM, U, 10, it + 2)
                    lo(Kl[:, :], kf, Kh[:, :]).then_inc(pool_fl, 1)
                if exists(n, 1, 32):
                    need(pool, act_ah, b, T_SLOT, U, SPU, s)
                    lo(Al[:, :, :].rearrange("p h t -> p (h t)"), of,
                       Ah[:, :, :].rearrange("p h t -> p (h t)")).then_inc(pool_al, 1)
                if s == 3 and exists(n, 2, 25):
                    wlo_a(b, U, A_PRO + 5, Wl[:, 1, :], Wh[:, 1, :])
                    wlo_a(b, U, A_PRO + 6, Wl[:, 2, :], Wh[:, 2, :])
                if s == 4 and exists(n, 2, 25):
                    wlo_a(b, U, A_PRO + 7, Wl[:, 3, :], Wh[:, 3, :])
                    wlo_a(b, U, A_PRO + 8, Wl[:, 4, :], Wh[:, 4, :])
                if s == 5 and exists(n, 2, 25):
                    wlo_a(b, U, A_PRO + 9, Wl[:, 5, :], Wh[:, 5, :])
                if s == 9 and exists(n, 2, 25):
                    for h in range(2, 4):
                        wlo_a(b, U + 1, A_PRO + h, Ol[:, h, :], Oh[:, h, :])
                if n == 1:
                    for h in range(2, 4):
                        wlo_a(b, 0, A_PRO + h, Ol[:, h, :], Oh[:, h, :])
                if n is not None and 28 <= n <= 31:
                    for i in (2 * (n - 28), 2 * (n - 28) + 1):
                        w = w_of_piece_f[i]
                        wlo_f(b, 0, i, Wl[:, w, :], Wh[:, w, :])

            def slot_f(b, U, s, n):
                deviations(jobs(b, 1, n))
                if s % 4 == 0 and exists(n, 4, 32):
                    d = s // 4 - 1
                    for i in range(2):
                        need(pool, act_hh, b, 8 * NU, U, 8, 4 * d + i + 1)
                        lo(big_l[:, d % 2, i, :], hid[:, i, :], big_h[:, d % 2, i, :]).then_inc(pool_hl, 1)
                deviations([job for job in jobs(b, 1, n) if job[0] == "mid"], second=True)
                if n == 1:
                    pool.wait_ge(pe_xt, turned("mid", b, TT))
                    pool.memset(YF, 0.0).then_inc(yf_ok, 2)
                if b + 1 < B and n == 33:
                    wlo_a(b + 1, 0, 0, Wl[:, 0, :], Wh[:, 0, :])
                if s == 5 and exists(n, 5, 29):
                    for i in range(4):
                        wlo_f(b, U, F_PRO + i, Ol[:, i, :], Oh[:, i, :])
                if 5 <= s <= 8 and exists(n, 5, 28):
                    i = s - 5
                    wlo_f(b, U, F_PRO + 4 + 2 * i, Wl[:, i, :], Wh[:, i, :])
                    wlo_f(b, U, F_PRO + 5 + 2 * i, Wl[:, 4 + i, :], Wh[:, 4 + i, :])

            pool.wait_ge(const_ok, 1)
            first = [("in", 0, t) for t in range(4)]
            deviations(first[0:2])
            wlo_a(0, 0, 0, Wl[:, 0, :], Wh[:, 0, :])
            deviations(first[2:4])
            for b in range(B):
                walk_a(pool, b, slot_a)
                walk_f(pool, b, slot_f)
            deviations(jobs(B, 0, -5))


_OUT = ((B, S, DM), "float32")


def kernel(L0_attn_x, L0_attn_Wq, L0_attn_Wk, L0_attn_Wv, L0_attn_Wo,
           L0_ffn_w_gate, L0_ffn_w_up, L0_ffn_w_down):
    import concourse.bacc as bacc
    from concourse.bass_utils import run_bass_kernel_spmd

    def f(a):
        return np.ascontiguousarray(a)

    Wq = np.asarray(L0_attn_Wq).reshape(KVH, REP, P, KT, P).transpose(0, 1, 4, 3, 2)
    Wk = np.asarray(L0_attn_Wk).reshape(KVH, P, KT, P).transpose(0, 3, 2, 1)
    Wv = np.asarray(L0_attn_Wv).reshape(KVH, P, KT, P).transpose(0, 3, 2, 1)
    Wo = np.asarray(L0_attn_Wo).reshape(DM, KVH, REP, P).transpose(1, 2, 3, 0)
    Wg = np.asarray(L0_ffn_w_gate).reshape(KT, P, NU, P, 4).transpose(2, 4, 1, 0, 3)
    Wu = np.asarray(L0_ffn_w_up).reshape(KT, P, NU, P, 4).transpose(2, 4, 1, 0, 3)
    Wd = np.asarray(L0_ffn_w_down).reshape(NU, P, 4, DM).transpose(0, 2, 1, 3)
    power = np.arange(0, P, 2, dtype=np.float32) / np.float32(P)
    freq = np.float32(1) / np.power(10000.0, power.astype(np.float64)).astype(np.float32)
    angle = np.outer(freq, np.arange(S, dtype=np.float32)).astype(np.float64)
    cos = np.cos(angle).astype(np.float32)
    sin = np.sin(angle).astype(np.float32)
    place = np.arange(P)
    arrays = {
        "x": f(L0_attn_x),
        "wq": f(Wq).reshape(NU, 4, P, W), "wk": f(Wk).reshape(NU, P, W), "wv": f(Wv).reshape(NU, P, W),
        "wo": f(Wo), "wg": f(Wg).reshape(NU, 4, P, W), "wu": f(Wu).reshape(NU, 4, P, W), "wd": f(Wd),
        "cos_t": np.concatenate([cos, cos]), "sin_t": np.concatenate([-sin, sin]),
        "causal": (place[:, None] <= place[None, :]).astype(np.float32),
        "eye": np.eye(P, dtype=np.float32),
    }
    nc = bacc.Bacc("TRN2", target_bir_lowering=False, num_devices=1)
    args = [nc.dram_tensor(n, a.shape, mybir.dt.from_np(a.dtype), kind="ExternalInput").ap()
            for n, a in arrays.items()]
    shape, dtype = _OUT
    args.append(nc.dram_tensor("out", shape, mybir.dt.from_np(np.dtype(dtype)), kind="ExternalOutput").ap())
    build(nc, *args)
    r = run_bass_kernel_spmd(nc, [arrays], core_ids=[0])
    return r.results[0]["out"]
```

```python
from contextlib import ExitStack

import numpy as np

import concourse.bass as bass
from concourse import mybir

ALU = mybir.AluOpType
ACT = mybir.ActivationFunctionType
F32 = mybir.dt.float32
F32R = mybir.dt.float32r
BF16 = mybir.dt.bfloat16

P = 128
B, S, DM = 2, 1024, 512
KVH, REP = 4, 4
W = 512
KT = DM // P
TT = S // P
HALF = P // 2
NU = 4
SPU = 8
EPS_LN = 1e-5
EPS_DEN = 1e-6
VP = P + 2

RING_A, RING_F = 5, 4
A_PRO, A_UNIT = 6, 10
F_PRO, F_UNIT = 8, 12

T_SLOT = NU * SPU
T_ITEM = 5 * 2 * NU
T_KV = 2 * 2 * NU
T_STEP = 2 * NU
T_STATE = 7 * NU
W_DVE = {0: 1, 1: 2, 4: 3}
W_POOL = {2: 1, 3: 2, 5: 3, 6: 4, 7: 5, 8: 6, 9: 7}
T_WPOOL_A = A_PRO + len(W_POOL) * (NU - 1) + 2
T_WDVE = len(W_DVE) * (NU - 1) + 2
T_WACT_A = A_PRO + 10 * (NU - 1) + 4
T_W_F = F_PRO + F_UNIT * (NU - 1) + 4


KINDS = ("in", "mid", "out")


def jobs(b, layer, n):
    if n is None:
        return []
    found = []
    if layer == 0:
        if b < B and n in (-5, -4):
            found += [("in", b, 4 + 2 * (n + 5)), ("in", b, 5 + 2 * (n + 5))]
        if b > 0 and n == -5:
            found.append(("out", b - 1, TT - 1))
        if b < B and 27 <= n <= 31:
            found.append(("mid", b, n - 27))
    else:
        if n in (0, 1, 2):
            found.append(("mid", b, 5 + n))
        if b + 1 < B and n == 29:
            found += [("in", b + 1, 0), ("in", b + 1, 1)]
        if b + 1 < B and n in (30, 31):
            found.append(("in", b + 1, n - 28))
        if 30 <= n <= 36:
            found.append(("out", b, n - 30))
    return found


def jobs_before(b, layer, n):
    if n is None:
        return []
    if layer == 0 and n == -5:
        found = jobs(b - 1, 1, 36) if b > 0 else []
    elif layer == 1 and n == 0:
        found = jobs(b, 0, 33)
    else:
        found = jobs(b, layer, n - 1)
    return [job for job in found if job[0] != "out"]


def turned(kind, b, t):
    return b * 2 * TT + (TT if kind == "mid" else 0) + t


def item_of(m):
    return m + 5 + max(0, (m + 1) // 4 + (1 if m >= -1 else 0))


def key_item_of(m):
    return item_of(m) + 1


def build(nc, x, wq, wk, wv, wo, wg, wu, wd, cos_t, sin_t, causal, eye, out):
    with ExitStack() as ctx:
        def sb(name, shape, dtype=F32):
            return ctx.enter_context(nc.sbuf_tensor(name, shape, dtype))

        def sem(name):
            return ctx.enter_context(nc.semaphore(name))

        Xh = sb("x_hi", [P, KT, S], F32R)
        Xl = sb("x_lo", [P, KT, S], F32R)
        Y = sb("y_acc", [P, TT, DM])
        Wh = sb("w_hi", [P, 8, W], F32R)
        Wl = sb("w_lo", [P, 8, W], F32R)
        Oh = sb("wout_hi", [P, 4, W], F32R)
        Ol = sb("wout_lo", [P, 4, W], F32R)
        stage = sb("stage", [P, RING_A, W])
        big_h = sb("big_hi", [P, 2, 4, W], F32R)
        big_l = sb("big_lo", [P, 2, 4, W], F32R)
        Kh = sb("k_hi", [P, W], F32R)
        Kl = sb("k_lo", [P, W], F32R)
        KTh = sb("kt_hi", [P, 4, P], F32R)
        KTl = sb("kt_lo", [P, 4, P], F32R)
        Vh = sb("v_hi", [P, 4, VP], F32R)
        Vl = sb("v_lo", [P, 4, P], F32R)
        Sh = [sb("s_hi", [P, W], F32R)[:, :], Wh[:, 6, :]]
        Sl = [sb("s_lo", [P, W], F32R)[:, :], Wl[:, 6, :]]
        Ah = sb("a_hi", [P, 4, P], F32R)
        Al = sb("a_lo", [P, 4, P], F32R)
        Sth = sb("st_hi", [P, 2, P], F32R)
        Stl = sb("st_lo", [P, 2, P], F32R)
        ones = sb("ones", [P, P], F32R)
        mask = sb("mask", [P, P])
        ident = sb("ident", [P, P])
        scr = sb("scratch", [P, 18, W])
        msk = sb("masks", [P, 6, W], BF16)
        xr = sb("x_rows", [P, 2, W])
        small = sb("small", [P, 64])
        mhalf, eps_den, eps_ln = [small[:, i:i + 1] for i in range(3)]
        stat, mv, rstd = {}, {}, {}
        for i, kind in enumerate(KINDS):
            at = 4 + 20 * i
            stat[kind] = small[:, at:at + 12].rearrange("p (k c) -> p k c", k=2)
            mv[kind] = small[:, at + 12:at + 16].rearrange("p (k c) -> p k c", k=2)
            rstd[kind] = small[:, at + 16:at + 18]

        rot, xq, Eq, fq, vT, xk, Ek, kf, Sf, r0, Tn, of = [scr[:, i, :] for i in range(12)]
        cosb = scr[:, 12:14, :]
        sinb = scr[:, 14:16, :]
        YF = scr[:, 0:8, :]
        hid = scr[:, 8:12, :]
        ab = scr[:, 12:16, :]
        sg = scr[:, 16, :]
        Wmax = [scr[:, 17, :], ab[:, 1, :]]
        c01, c23, pw, qw, rr, m2 = [msk[:, i, :] for i in range(6)]
        m0 = qw
        def xt_in(b, t):
            if b == 0 or t >= 4:
                return scr[:, 4 + t, :]
            return stage[:, 4, :] if t == 2 else xr[:, t % 2, :]

        xn_mid = [scr[:, 0, :], scr[:, 1, :]]

        bank = [ctx.enter_context(nc.psum_tensor(f"bank{i}", [P, W], F32)) for i in range(8)]
        psS, psQ, psK, psO, psD, psY, psSt, psT = bank
        psG, psU, psYF = bank[0:2], [bank[3], bank[2]], bank[4:6]

        def psX(kind, t):
            return ([psK, psT] if kind == "mid" and t < 4 else bank[6:8])[t % 2]


        ident_ld = sem("ident_ld")
        mask_ld = sem("mask_ld")
        const_ok = sem("const_ok")
        tab_ld = sem("tab_ld")
        ld_a = [sem(f"ld_a{i}") for i in range(RING_A)]
        ld_f = [sem(f"ld_f{i}") for i in range(RING_F)]
        act_w = sem("act_w")
        pool_w = sem("pool_w")
        dve_w = sem("dve_w")
        act_wf = sem("act_wf")
        pool_wf = sem("pool_wf")
        ld_in = [sem(f"ld_in{t}") for t in range(TT)]
        ld_mid = [sem(f"ld_mid{i}") for i in range(2)]
        st_out = sem("st_out")
        dve_stat = {kind: sem(f"dve_stat_{kind}") for kind in KINDS}
        dve_var = {kind: sem(f"dve_var_{kind}") for kind in KINDS}
        pool_rs = {kind: sem(f"pool_rs_{kind}") for kind in KINDS}
        pool_eps = sem("pool_eps")
        dve_norm = {kind: sem(f"dve_norm_{kind}") for kind in KINDS[1:]}
        dve_xn = sem("dve_xn")
        pe_xt = sem("pe_xt")
        act_xh = sem("act_xh")
        dve_xl = sem("dve_xl")
        dve_res = sem("dve_res")
        pool_out = sem("pool_out")
        dve_self = sem("dve_self")
        dve_const = sem("dve_const")
        pe_q = sem("pe_q")
        pe_kv = sem("pe_kv")
        pe_tr = sem("pe_tr")
        pe_s = sem("pe_s")
        pe_pv = sem("pe_pv")
        pe_st = sem("pe_st")
        pe_y = sem("pe_y")
        act_rot = sem("act_rot")
        act_exp = sem("act_exp")
        act_fh = sem("act_fh")
        act_vt = sem("act_vt")
        act_kvh = sem("act_kvh")
        act_ln = sem("act_ln")
        act_r0 = sem("act_r0")
        act_sh = sem("act_sh")
        act_sth = sem("act_sth")
        act_ah = sem("act_ah")
        dve_t1 = sem("dve_t1")
        dve_t2 = sem("dve_t2")
        dve_x = sem("dve_x")
        dve_m = sem("dve_m")
        dve_f = sem("dve_f")
        dve_sf = sem("dve_sf")
        dve_T = sem("dve_T")
        dve_U = sem("dve_U")
        dve_a = sem("dve_a")
        dve_kvl = sem("dve_kvl")
        dve_stl = sem("dve_stl")
        y_ok = sem("y_ok")
        pool_fl = sem("pool_fl")
        pool_sl = sem("pool_sl")
        pool_al = sem("pool_al")
        pe_g = sem("pe_g")
        pe_u = sem("pe_u")
        pe_d = sem("pe_d")
        act_sg = sem("act_sg")
        act_ab = sem("act_ab")
        act_hh = sem("act_hh")
        dve_h = sem("dve_h")
        dve_rank = sem("dve_rank")
        dve_hs = sem("dve_hs")
        dve_hl = sem("dve_hl")
        yf_ok = sem("yf_ok")
        pool_hl = sem("pool_hl")

        block = ctx.enter_context(nc.Block())

        def need(eng, s, b, total, U, per_unit, k):
            if isinstance(U, int):
                k, U = k + U * per_unit, None
                if k <= 0:
                    return
                eng.wait_ge(s, b * total + k)
            else:
                assert k > 0
                eng.wait_ge(s, b * total + U * per_unit + k)

        def first_a_pieces(b, layer, n):
            if n is None or (layer == 0 and n >= 0):
                return []
            if b == 0:
                return [n + 6] if layer == 0 else []
            if layer == 1:
                return [n - 30] if b < B and 30 <= n <= 33 else []
            return [n + 9] if n <= -4 else []

        def first_f(layer, n):
            if layer == 0:
                return [n - 28] if n is not None and n >= 28 else []
            return [6, 7] if n == 0 else []

        w_of_piece_f = [0, 4, 1, 5, 2, 6, 3, 7]

        def q_tile(n):
            return {-4: psS, -3: psO, -2: psD}.get(n, psQ)

        def walk_a(eng, b, slot):
            for s in range(-5, 2):
                slot(b, 0, s, s)
            with eng.Fori(0, NU - 1) as U:
                for s in range(2, 2 + SPU):
                    slot(b, U, s, None)
            for s in range(2, 2 + SPU):
                slot(b, NU - 1, s, SPU * (NU - 1) + s)

        def walk_f(eng, b, slot):
            for s in range(0, 5):
                slot(b, 0, s, s)
            with eng.Fori(0, NU - 1) as U:
                for s in range(5, 5 + SPU):
                    slot(b, U, s, None)
            for s in range(5, 5 + SPU):
                slot(b, NU - 1, s, SPU * (NU - 1) + s)

        def exists(n, low, high):
            return n is None or low <= n <= high

        @block.sync
        def _(sp):
            def x_in(b, t):
                if b > 0:
                    if t >= 6:
                        sp.wait_ge(dve_hl, b * 4 * NU)
                    elif t >= 4:
                        sp.wait_ge(pool_hl, b * 4 * NU)
                    elif t == 3:
                        sp.wait_ge(pe_xt, turned("in", b, 1) + 1)
                    else:
                        sp.wait_ge(dve_res, b * TT)
                sp.dma_start(xt_in(b, t), x[b, t * P:(t + 1) * P, :]).then_inc(ld_in[t], 16)

            def x_mid(b, t):
                if t >= 2:
                    sp.wait_ge(dve_res, b * TT + t - 1)
                elif b > 0:
                    sp.wait_ge(pe_xt, turned("in", b, TT))
                sp.dma_start(xr[:, t % 2, :], x[b, t * P:(t + 1) * P, :]).then_inc(ld_mid[t % 2], 16)

            def tables(b):
                if b > 0:
                    sp.wait_ge(dve_hs, b * 8 * NU)
                sp.dma_start(cosb, cos_t.rearrange("p (a t) -> p a t", a=2)).then_inc(tab_ld, 16)
                sp.dma_start(sinb, sin_t.rearrange("p (a t) -> p a t", a=2)).then_inc(tab_ld, 16)

            def piece_a(b, U, i, src):
                before = i - RING_A
                r, u = before - A_PRO, U
                if i >= A_PRO and r < 0 and not (isinstance(U, int) and U == 0):
                    r, u = r + A_UNIT, U - 1
                if i < A_PRO or r < 0:
                    if before >= 0:
                        sp.wait_ge(pool_w, b * T_WPOOL_A + before + 1)
                elif r in W_DVE:
                    sp.wait_ge(dve_w, b * T_WDVE + 3 * u + W_DVE[r])
                else:
                    sp.wait_ge(pool_w, b * T_WPOOL_A + A_PRO + 7 * u + W_POOL[r])
                if b > 0 and i == 4:
                    sp.wait_ge(pe_xt, turned("in", b, 2) + 1)
                sp.dma_start(stage[:, i % RING_A, :], src).then_inc(ld_a[i % RING_A], 16)

            def unit_a(b, U, last):
                for j in range(4):
                    piece_a(b, U, A_PRO + j, wo[U, j])
                if not last:
                    for i, src in enumerate([wq[U + 1, 0], wq[U + 1, 1], wq[U + 1, 2], wq[U + 1, 3],
                                             wk[U + 1], wv[U + 1]]):
                        piece_a(b, U, A_PRO + 4 + i, src)

            def piece_f(b, U, i, src):
                if i >= RING_F:
                    sp.wait_ge(pool_wf, b * T_W_F + F_UNIT * U + i - RING_F + 1)
                sp.dma_start(stage[:, i % RING_F, :], src).then_inc(ld_f[i % RING_F], 16)

            def piece_f0(b, i):
                piece_f(b, 0, i, (wg, wu)[i % 2][0, i // 2])

            def unit_f(b, U, last):
                for j in range(4):
                    piece_f(b, U, F_PRO + j, wd[U, j])
                if not last:
                    for j in range(4):
                        piece_f(b, U, F_PRO + 4 + 2 * j, wg[U + 1, j])
                        piece_f(b, U, F_PRO + 5 + 2 * j, wu[U + 1, j])

            def store(b, t):
                sp.wait_ge(pool_out, b * TT + t + 1)
                sp.dma_start(out[b, t * P:(t + 1) * P, :], Y[:, t, :]).then_inc(st_out, 16)

            first_a = [wq[0, 0], wq[0, 1], wq[0, 2], wq[0, 3], wk[0], wv[0]]
            for t in range(4):
                x_in(0, t)
                if t == 1:
                    sp.dma_start(ident[:, :], eye).then_inc(ident_ld, 16)
            for i in range(5):
                piece_a(0, 0, i, first_a[i])
                if i == 0:
                    sp.dma_start(mask[:, :], causal).then_inc(mask_ld, 16)
                if i < 4:
                    x_in(0, 4 + i)
            tables(0)
            piece_a(0, 0, 5, first_a[5])
            for b in range(B):
                unit_a(b, 0, False)
                with sp.Fori(1, NU - 1) as U:
                    unit_a(b, U, False)
                x_mid(b, 0)
                x_mid(b, 1)
                unit_a(b, NU - 1, True)
                sp.wait_ge(pool_w, (b + 1) * T_WPOOL_A)
                sp.wait_ge(dve_w, (b + 1) * T_WDVE)
                for i in range(4):
                    piece_f0(b, i)
                x_mid(b, 2)
                x_mid(b, 3)
                piece_f0(b, 4)
                piece_f0(b, 5)
                x_mid(b, 4)
                x_mid(b, 5)
                piece_f0(b, 6)
                piece_f0(b, 7)
                x_mid(b, 6)
                x_mid(b, 7)
                with sp.Fori(0, NU - 1) as U:
                    unit_f(b, U, False)
                if b + 1 == B:
                    unit_f(b, NU - 1, True)
                    for t in range(TT):
                        store(b, t)
                else:
                    for t in range(3):
                        x_in(b + 1, t)
                    unit_f(b, NU - 1, True)
                    sp.wait_ge(pool_wf, (b + 1) * T_W_F)
                    for i in range(4):
                        piece_a(b + 1, 0, i, first_a[i])
                    x_in(b + 1, 3)
                    store(b, 0)
                    piece_a(b + 1, 0, 4, first_a[4])
                    piece_a(b + 1, 0, 5, first_a[5])
                    store(b, 1)
                    for t in range(4, TT):
                        x_in(b + 1, t)
                    tables(b + 1)
                    for t in range(2, 4):
                        store(b, t)
                    for t in range(4, TT):
                        store(b, t)
            sp.wait_ge(st_out, B * TT * 16)

        @block.tensor
        def _(pe):
            def three(ps, whi, wlo, xhi, xlo, first, last):
                pe.matmul(ps, whi, xhi, start=first, stop=False, skip_group_check=True)
                pe.matmul(ps, wlo, xhi, start=False, stop=False, skip_group_check=True)
                return pe.matmul(ps, whi, xlo, start=False, stop=last, skip_group_check=True)

            def turn(kind, b, t):
                k = turned(kind, b, t)
                ps, xn = psX(kind, t), xt_in(b, t) if kind == "in" else xn_mid[t % 2]
                pe.wait_ge(dve_xn, k + 1)
                if k > 1:
                    pe.wait_ge(dve_xl, k - 1)
                if kind == "mid" and t == 0:
                    pe.wait_ge(act_vt, (b + 1) * T_STEP)
                if kind == "mid" and t == 1:
                    pe.wait_ge(dve_kvl, (b + 1) * T_KV)
                if kind == "mid" and t == 4:
                    pe.wait_ge(dve_stl, (b + 1) * T_STATE)
                for kk in range(KT):
                    ins = pe.transpose(ps[:, kk * P:(kk + 1) * P], xn[:, kk * P:(kk + 1) * P], ident[:, :])
                ins.then_inc(pe_xt, 1)

            def project(ps, w, step):
                for kk in range(KT):
                    ins = three(ps[:, :], Wh[:, w, kk * P:(kk + 1) * P], Wl[:, w, kk * P:(kk + 1) * P],
                                Xh[:, kk, step * W:(step + 1) * W], Xl[:, kk, step * W:(step + 1) * W],
                                kk == 0, kk == KT - 1)
                return ins

            def queries(b, U, s, n):
                j = (s + 1) % 4
                if n is not None and n < -1:
                    pe.wait_ge(pool_w, b * T_WPOOL_A + j + 1)
                elif s == 3:
                    need(pe, dve_w, b, T_WDVE, U, 3, W_DVE[4])
                elif 4 <= s <= 6:
                    need(pe, pool_w, b, T_WPOOL_A, U, 7, A_PRO + W_POOL[s + 1])
                if n is None or n >= 0:
                    need(pe, dve_t1, b, T_ITEM, U, 10, item_of(s - 1) + 1)
                elif n == -1:
                    need(pe, dve_t1, b, T_ITEM, U, 10, item_of(-5) + 1)
                elif n == -5:
                    pe.wait_ge(dve_xl, turned("in", b, 4))
                    if b > 0:
                        pe.wait_ge(act_sg, b * T_SLOT)
                        pe.wait_ge(dve_h, b * T_SLOT)
                elif n == -2 and b > 0:
                    pe.wait_ge(yf_ok, b * (T_SLOT + 2) - 1)
                project(q_tile(n), j, ((s + 1) // 4 + 1) % 2).then_inc(pe_q, 1)

            def keys(b, U, s, n):
                if n is not None and n < 0:
                    pe.wait_ge(pool_w, b * T_WPOOL_A + 5)
                elif s == 6:
                    need(pe, pool_w, b, T_WPOOL_A, U, 7, A_PRO + W_POOL[8])
                need(pe, act_vt, b, T_STEP, U, 2, (s + 2) // 4)
                project(psK, 4, ((s + 2) // 4) % 2).then_inc(pe_kv, 1)

            def scores(b, U, s, n):
                if s % 4 == 0:
                    need(pe, pool_fl, b, T_ITEM, U, 10, 5 * (s // 4) + 5)
                need(pe, dve_sf, b, T_SLOT, U, SPU, s)
                par, c = (s // 4) % 2, s % 4
                t = slice(c * P, (c + 1) * P)
                ins = three(psS[:, :].rearrange("p (h t) -> p h t", h=4), Kh[:, t], Kl[:, t],
                            big_h[:, par, :, t], big_l[:, par, :, t], True, True)
                ins.then_inc(pe_s, 1)

            def slot_a(b, U, s, n):
                if exists(n, 29, 31) and n is not None:
                    scores(b, U, s, n)
                if exists(n, 1, 32):
                    m = s - 1
                    mu, ms = m // SPU, m % SPU
                    par, c = (m // 4) % 2, m % 4
                    t = slice(c * P, (c + 1) * P)
                    need(pe, pool_sl, b, T_SLOT, U, SPU, m + 1)
                    if c == 0:
                        need(pe, dve_kvl, b, T_KV, U, 4, 2 * (m // 4) + 1)
                    need(pe, dve_a, b, T_SLOT, U, SPU, m)
                    o3 = psO[:, :].rearrange("p (h t) -> p h t", h=4)
                    d3 = psD[:, :].rearrange("p (h t) -> p h t", h=4)
                    first = ms == 0
                    three(psO[:, :], Vh[:, c, 0:P], Vl[:, c, :], Sh[m % 2], Sl[m % 2], True, first)
                    pe.matmul(psD[:, :], ones[:, :], Sh[m % 2], start=True, stop=False, skip_group_check=True)
                    ins = pe.matmul(psD[:, :], ones[:, :], Sl[m % 2], start=False, stop=first, skip_group_check=True)
                    if not first:
                        need(pe, dve_stl, b, T_STATE, U, 7, 7 * mu + ms)
                        three(o3, Sth[:, 0, :], Stl[:, 0, :], big_h[:, par, :, t], big_l[:, par, :, t], False, True)
                        ins = three(d3, Sth[:, 1, :], Stl[:, 1, :], big_h[:, par, :, t], big_l[:, par, :, t],
                                    False, True)
                    ins.then_inc(pe_pv, 1)
                    if ms < SPU - 1:
                        if c == 0:
                            need(pe, dve_kvl, b, T_KV, U, 4, 2 * (m // 4) + 2)
                        if first:
                            need(pe, dve_stl, b, T_STATE, U, 7, 7 * mu)
                        pe.matmul(psSt[:, 0:VP], KTh[:, c, :], Vh[:, c, :], start=first, stop=False,
                                  skip_group_check=True)
                        pe.matmul(psSt[:, 0:VP], KTl[:, c, :], Vh[:, c, :], start=False, stop=False,
                                  skip_group_check=True)
                        pe.matmul(psSt[:, 0:P], KTh[:, c, :], Vl[:, c, :], start=False, stop=True,
                                  skip_group_check=True).then_inc(pe_st, 1)
                if s % 4 == 0 and exists(n, 0, 28):
                    need(pe, act_vt, b, T_STEP, U, 2, s // 4 + 1)
                    need(pe, dve_kvl, b, T_KV, U, 4, 2 * (s // 4))
                    for c in range(4):
                        ins = pe.transpose(psT[:, c * P:(c + 1) * P], vT[:, c * P:(c + 1) * P], ident[:, :])
                    ins.then_inc(pe_tr, 1)
                if n == -1:
                    pe.wait_ge(dve_xl, turned("in", b, TT))
                if n == 32:
                    pe.wait_ge(dve_xl, turned("mid", b, 4))
                    pe.wait_ge(dve_sf, (b + 1) * T_SLOT)
                    pe.wait_ge(pool_wf, b * T_W_F + 1)
                    project(psG[0], 0, 0).then_inc(pe_g, 1)
                if exists(n, 0, 28):
                    scores(b, U, s, n)
                if n is not None and n >= 0:
                    for kind, jb, t in jobs_before(b, 0, n):
                        turn(kind, jb, t)
                if exists(n, 2, 33):
                    need(pe, pool_al, b, T_SLOT, U, SPU, s - 1)
                    need(pe, y_ok, b, T_SLOT + 1, U, SPU, s - 1)
                    for h in range(4):
                        if s == 2:
                            if h < 2:
                                need(pe, dve_w, b, T_WDVE, U, 3, W_DVE[h])
                            else:
                                need(pe, pool_w, b, T_WPOOL_A, U, 7, A_PRO + W_POOL[h])
                        ins = three(psY[:, :], Ah[:, h, :], Al[:, h, :], Oh[:, h, :], Ol[:, h, :], h == 0, h == 3)
                    ins.then_inc(pe_y, 1)
                if s % 4 == 0 and exists(n, 0, 28):
                    need(pe, dve_kvl, b, T_KV, U, 4, 2 * (s // 4) + 1)
                    for c in range(4):
                        ins = pe.transpose(psT[:, c * P:(c + 1) * P], kf[:, c * P:(c + 1) * P], ident[:, :])
                    ins.then_inc(pe_tr, 1)
                if exists(n, -5 if b == 0 else -1, 26):
                    queries(b, U, s, n)
                if n == -4 and b > 0:
                    queries(b, 0, -2, -2)
                    keys(b, 0, -2, -2)
                if s % 4 == 2 and exists(n, -2 if b == 0 else -1, 26):
                    keys(b, U, s, n)
                if s % 4 == 3 and exists(n, -1, 27):
                    if n is not None and n < 0:
                        pe.wait_ge(pool_w, b * T_WPOOL_A + 6)
                    elif s == 7:
                        need(pe, pool_w, b, T_WPOOL_A, U, 7, A_PRO + W_POOL[9])
                    need(pe, dve_t1, b, T_ITEM, U, 10, key_item_of(s - 1) + 1)
                    project(psK, 5, ((s + 1) // 4) % 2).then_inc(pe_kv, 1)
                if n is not None and n < 0:
                    for kind, jb, t in jobs_before(b, 0, n):
                        turn(kind, jb, t)

            def slot_f(b, U, s, n):
                j = s % 4
                if n == 0:
                    pe.wait_ge(dve_t1, (b + 1) * T_ITEM)
                    pe.wait_ge(dve_a, (b + 1) * T_SLOT)
                if n == 1:
                    pe.wait_ge(dve_xl, turned("mid", b, 3))
                if n == 4:
                    pe.wait_ge(dve_xl, turned("mid", b, TT))
                if n == 5:
                    pe.wait_ge(y_ok, (b + 1) * (T_SLOT + 1))
                if exists(n, 0, 31):
                    if n is not None and n < 4:
                        pe.wait_ge(pool_wf, b * T_W_F + 2 * j + 2)
                    elif s >= 8 and s < 12:
                        need(pe, pool_wf, b, T_W_F, U, F_UNIT, F_PRO + 4 + 2 * j + 2)
                    if n != 0:
                        need(pe, act_sg, b, T_SLOT, U, SPU, s - 1)
                        project(psG[s % 2], j, (s // 4) % 2).then_inc(pe_g, 1)
                    need(pe, dve_h, b, T_SLOT, U, SPU, s - 1)
                    project(psU[s % 2], 4 + j, (s // 4) % 2).then_inc(pe_u, 1)
                for kind, jb, t in jobs_before(b, 1, n):
                    turn(kind, jb, t)
                if exists(n, 5, 36):
                    y = s - 5
                    d, ts = y // 4, y % 4
                    need(pe, yf_ok, b, T_SLOT + 2, U, SPU, y + 1)
                    for i in range(4):
                        if ts == 0 and i < 2:
                            need(pe, pool_hl, b, 4 * NU, U, 4, 2 * d + i + 1)
                        elif ts == 0:
                            need(pe, dve_hl, b, 4 * NU, U, 4, 2 * d + i - 1)
                        if s == 5:
                            need(pe, pool_wf, b, T_W_F, U, F_UNIT, F_PRO + i + 1)
                        ins = three(psYF[y % 2][:, :], big_h[:, d % 2, i, ts * P:(ts + 1) * P],
                                    big_l[:, d % 2, i, ts * P:(ts + 1) * P], Oh[:, i, :], Ol[:, i, :],
                                    i == 0, i == 3)
                    ins.then_inc(pe_d, 1)
                if n == 32 and b + 1 < B:
                    for q in (-5, -4, -3):
                        queries(b + 1, 0, q, q)

            pe.wait_ge(const_ok, 1)
            pe.wait_ge(ident_ld, 16)
            for t in range(4):
                turn("in", 0, t)
            for b in range(B):
                walk_a(pe, b, slot_a)
                walk_f(pe, b, slot_f)

        @block.scalar
        def _(act):
            copy = nc.scalar.copy

            def split_x(kind, b, t):
                ps = psX(kind, t)
                act.wait_ge(pe_xt, turned(kind, b, t) + 1)
                copy(Xh[:, :, t * P:(t + 1) * P], ps[:, :].rearrange("p (c t) -> p c t", c=KT)).then_inc(act_xh, 1)

            def raw(b, ring, lds, i, U, per_unit, total):
                slot_ = i % ring
                k = i // ring + 1
                act.wait_ge(lds[slot_], (b * total + U * (per_unit // ring) + k) * 16)
                return stage[:, slot_, :]

            def count_a(slot_):
                return sum(1 for i in range(T_WACT_A) if i % RING_A == slot_)

            def count_f(slot_):
                return sum(1 for i in range(T_W_F) if i % RING_F == slot_)

            def wsplit_a(b, U, i, dst):
                copy(dst, raw(b, RING_A, ld_a, i, U, A_UNIT, count_a(i % RING_A))).then_inc(act_w, 1)

            def wsplit_f(b, U, i, dst):
                copy(dst, raw(b, RING_F, ld_f, i, U, F_UNIT, count_f(i % RING_F))).then_inc(act_wf, 1)

            def turn_half(src):
                def to(dst):
                    copy(dst[HALF:P, :], src[0:HALF, :])
                    return copy(dst[0:HALF, :], src[HALF:P, :])
                return to

            def split_scores(b, U, s):
                need(act, dve_sf, b, T_SLOT, U, SPU, s + 1)
                need(act, pe_pv, b, T_SLOT, U, SPU, s - 1)
                copy(Sh[s % 2], Sf).then_inc(act_sh, 1)

            def slot_a(b, U, s, n):
                for i in first_a_pieces(b, 0, n):
                    wsplit_a(b, 0, i, Wh[:, i, :])
                m = s - 1
                mu, ms = m // SPU, m % SPU
                it = item_of(m)
                q_item = exists(n, -4, 27)
                k_item = m % 4 == 2 and exists(n, -1, 27)
                if n == -5:
                    nc.scalar.preload_act_table_set("natural_log_exp_and_others")
                if n == -4 and b > 0:
                    act.wait_ge(pool_out, b * TT - 4)
                if n == -1 and b > 0:
                    act.wait_ge(pool_out, b * TT)
                if q_item:
                    need(act, pe_q, b, T_SLOT, U, SPU, m + 6)
                    need(act, dve_x, b, T_ITEM, U, 10, it)
                    turn_half(q_tile(n and n - 1))(rot).then_inc(act_rot, 1)
                if k_item:
                    need(act, pe_kv, b, T_KV, U, 4, 2 * ((s + 1) // 4) + 1)
                    need(act, pe_tr, b, T_KV, U, 4, 2 * ((s + 1) // 4))
                    turn_half(psK)(vT).then_inc(act_rot, 1)
                if n is not None and 29 <= n <= 31:
                    split_scores(b, U, s)
                if exists(n, 1, 32) and ms < SPU - 1:
                    need(act, pe_st, b, T_STATE, U, 7, 7 * mu + ms + 1)
                    copy(Sth[:, 0, :], psSt[:, 0:P])
                    copy(Sth[:, 1, :], psSt[:, P:P + 1].to_broadcast([P, P])).then_inc(act_sth, 1)
                if exists(n, 1, 32):
                    need(act, pe_pv, b, T_SLOT, U, SPU, s)
                    need(act, dve_U, b, T_SLOT, U, SPU, s - 1)
                    nc.scalar.activation(r0, psD[:, :], ACT.Ln, bias=eps_den[:, 0:1]).then_inc(act_ln, 1)
                if q_item:
                    need(act, dve_x, b, T_ITEM, U, 10, it + 1)
                    nc.scalar.activation(Eq, xq, ACT.Exp).then_inc(act_exp, 1)
                if s % 4 == 0 and exists(n, 0, 28):
                    need(act, pe_tr, b, T_KV, U, 4, 2 * (s // 4) + 1)
                    copy(Vh[:, :, 0:P], psT[:, :].rearrange("p (c d) -> p c d", c=4)).then_inc(act_kvh, 1)
                if exists(n, 1, 32):
                    need(act, act_ln, b, T_SLOT, U, SPU, s)
                    nc.scalar.activation(r0, r0, ACT.Exp, scale=-1.0).then_inc(act_r0, 1)
                if k_item:
                    need(act, dve_x, b, T_ITEM, U, 10, it + 2)
                    nc.scalar.activation(Ek, xk, ACT.Exp).then_inc(act_exp, 1)
                if exists(n, 0, 28):
                    split_scores(b, U, s)
                for job in jobs_before(b, 0, n):
                    split_x(*job)
                if q_item:
                    need(act, dve_f, b, T_ITEM, U, 10, it + 1)
                    if m >= 3 or n is None:
                        need(act, pe_pv, b, T_SLOT, U, SPU, s)
                    copy(big_h[:, ((m + 1) // 4 + 1) % 2, (m + 1) % 4, :], fq).then_inc(act_fh, 1)
                if k_item:
                    need(act, dve_f, b, T_ITEM, U, 10, it + 2)
                    if m >= 2:
                        need(act, pe_s, b, T_SLOT, U, SPU, s + 1)
                    copy(Kh[:, :], kf).then_inc(act_fh, 1)
                if exists(n, 1, 32):
                    need(act, dve_a, b, T_SLOT, U, SPU, s)
                    need(act, pe_y, b, T_SLOT, U, SPU, s - 1)
                    copy(Ah[:, :, :].rearrange("p h t -> p (h t)"), of).then_inc(act_ah, 1)
                if s == 2 and exists(n, 2, 25):
                    need(act, pe_q, b, T_SLOT, U, SPU, 5)
                    wsplit_a(b, U, A_PRO + 4, Wh[:, 0, :])
                if s == 3 and exists(n, 2, 25):
                    need(act, pe_q, b, T_SLOT, U, SPU, 7)
                    wsplit_a(b, U, A_PRO + 5, Wh[:, 1, :])
                    wsplit_a(b, U, A_PRO + 6, Wh[:, 2, :])
                if s == 4 and exists(n, 2, 25):
                    need(act, pe_q, b, T_SLOT, U, SPU, 8)
                    wsplit_a(b, U, A_PRO + 7, Wh[:, 3, :])
                    need(act, pe_kv, b, T_KV, U, 4, 3)
                    wsplit_a(b, U, A_PRO + 8, Wh[:, 4, :])
                if s == 5 and exists(n, 2, 25):
                    need(act, pe_kv, b, T_KV, U, 4, 4)
                    wsplit_a(b, U, A_PRO + 9, Wh[:, 5, :])
                if s == 9 and exists(n, 2, 25):
                    need(act, pe_y, b, T_SLOT, U, SPU, s - 1)
                    for h in range(4):
                        wsplit_a(b, U + 1, A_PRO + h, Oh[:, h, :])
                if n == 1:
                    for h in range(4):
                        wsplit_a(b, 0, A_PRO + h, Oh[:, h, :])
                if s % 4 == 3 and exists(n, -1, 27):
                    need(act, pe_kv, b, T_KV, U, 4, 2 * ((s + 1) // 4) + 2)
                    need(act, dve_x, b, T_ITEM, U, 10, it + 2)
                    copy(vT, psK[:, :]).then_inc(act_vt, 1)
                if s % 4 == 0 and exists(n, 0, 28):
                    need(act, pe_tr, b, T_KV, U, 4, 2 * (s // 4) + 2)
                    copy(KTh[:, :, :].rearrange("p c d -> p (c d)"), psT[:, :]).then_inc(act_kvh, 1)
                if n == 28:
                    act.wait_ge(pe_kv, (b + 1) * T_KV)
                if n == 33:
                    act.wait_ge(pe_pv, (b + 1) * T_SLOT)
                for i in first_f(0, n):
                    wsplit_f(b, 0, i, Wh[:, w_of_piece_f[i], :])

            def slot_f(b, U, s, n):
                j = s % 4
                if s == 5 and exists(n, 5, 29):
                    need(act, pe_g, b, T_SLOT, U, SPU, s + 1)
                    for i in range(4):
                        wsplit_f(b, U, F_PRO + i, Oh[:, i, :])
                if 5 <= s <= 8 and exists(n, 5, 28):
                    i = s - 5
                    need(act, pe_u, b, T_SLOT, U, SPU, s)
                    wsplit_f(b, U, F_PRO + 4 + 2 * i, Wh[:, i, :])
                    wsplit_f(b, U, F_PRO + 5 + 2 * i, Wh[:, 4 + i, :])
                for i in first_a_pieces(b + 1, 1, n):
                    act.wait_ge(pe_u, b * T_SLOT + 28 + i + 1)
                    wsplit_a(b + 1, 0, i, Wh[:, i, :])
                if exists(n, 1, 32):
                    i = (s - 1) % 4
                    need(act, dve_h, b, T_SLOT, U, SPU, s)
                    need(act, dve_rank, b, T_STEP, U, 2, (s - 1) // 4)
                    nc.scalar.activation(ab[:, i, :], hid[:, i, :], ACT.Abs).then_inc(act_ab, 1)
                for i in first_f(1, n):
                    wsplit_f(b, 0, i, Wh[:, w_of_piece_f[i], :])
                if exists(n, 0, 31):
                    need(act, pe_g, b, T_SLOT, U, SPU, s + 1)
                    need(act, dve_h, b, T_SLOT, U, SPU, s)
                    nc.scalar.activation(sg, psG[s % 2][:, :], ACT.Silu).then_inc(act_sg, 1)
                for job in jobs_before(b, 1, n):
                    split_x(*job)
                if j == 0 and exists(n, 4, 32):
                    d = s // 4 - 1
                    for i in range(4):
                        need(act, dve_hs, b, 8 * NU, U, 8, 4 * d + i + 1)
                        copy(big_h[:, d % 2, i, :], hid[:, i, :]).then_inc(act_hh, 1)

            act.wait_ge(const_ok, 1)
            wsplit_a(0, 0, 0, Wh[:, 0, :])
            for t in range(4):
                split_x("in", 0, t)
            for b in range(B):
                walk_a(act, b, slot_a)
                walk_f(act, b, slot_f)

        @block.vector
        def _(dve):
            def source(kind, b, t):
                return {"in": xt_in(b, t), "mid": Y[:, t, :], "out": YF[:, t, :]}[kind]

            def count(kind, b, t, second=False):
                return (b * TT + t) * (2 if kind == "mid" else 1) + second

            def variances(todo, second=False):
                for kind, b, t in todo:
                    if kind == "in":
                        dve.wait_ge(ld_in[t], (b + 1) * 16)
                    elif kind == "out":
                        dve.wait_ge(yf_ok, b * (T_SLOT + 2) + 2 + 24 + t + 1)
                    elif second:
                        dve.wait_ge(dve_res, b * TT + t + 1)
                    else:
                        dve.wait_ge(y_ok, b * (T_SLOT + 1) + 1 + 24 + t + 1)
                    dve.bn_stats(stat[kind][:, t % 2, :], source(kind, b, t)).then_inc(dve_stat[kind], 1)
                for kind, b, t in todo:
                    dve.wait_ge(dve_stat[kind], count(kind, b, t, second) + 1)
                    dve.bn_aggr(mv[kind][:, t % 2, :], stat[kind][:, t % 2, :]).then_inc(dve_var[kind], 1)

            def normalise(kind, b, t, dst, second=False):
                k = count(kind, b, t, second)
                dve.wait_ge(pool_rs[kind], k + 1)
                dve.wait_ge(dve_var[kind], k + 1)
                return dve.tensor_scalar(dst, source(kind, b, t), mv[kind][:, t % 2, 0:1],
                                         rstd[kind][:, t % 2:t % 2 + 1], ALU.subtract, ALU.mult)

            def middle(todo):
                todo = [job for job in todo if job[0] != "in"]
                for kind, b, t in todo:
                    normalise(kind, b, t, source(kind, b, t)).then_inc(dve_norm[kind], 1)
                for kind, b, t in todo:
                    if kind == "mid":
                        dve.wait_ge(dve_norm[kind], b * TT + t + 1)
                        dve.wait_ge(ld_mid[t % 2], (b * TT + t) // 2 * 16 + 16)
                        dve.tensor_tensor(Y[:, t, :], Y[:, t, :], xr[:, t % 2, :], ALU.add).then_inc(dve_res, 1)
                variances([job for job in todo if job[0] == "mid"], second=True)

            def late(todo):
                for kind, b, t in todo:
                    if kind != "out":
                        xn = xt_in(b, t) if kind == "in" else xn_mid[t % 2]
                        normalise(kind, b, t, xn, second=kind == "mid").then_inc(dve_xn, 1)

            def split_x(kind, b, t):
                ps = psX(kind, t)
                dve.wait_ge(act_xh, turned(kind, b, t) + 1)
                dve.tensor_tensor(Xl[:, :, t * P:(t + 1) * P], ps[:, :].rearrange("p (c t) -> p c t", c=KT),
                                  Xh[:, :, t * P:(t + 1) * P].bitcast(F32), ALU.subtract).then_inc(dve_xl, 1)

            def wlo_a(b, U, r, dst, hi):
                need(dve, act_w, b, T_WACT_A, U, A_UNIT, A_PRO + r + 1)
                dve.tensor_tensor(dst, stage[:, (A_PRO + r) % RING_A, :], hi.bitcast(F32),
                                  ALU.subtract).then_inc(dve_w, 1)

            def mask_scores(b, U, s, n):
                if n == 0:
                    dve.wait_ge(mask_ld, 16)
                need(dve, pe_s, b, T_SLOT, U, SPU, s + 1)
                need(dve, pool_sl, b, T_SLOT, U, SPU, s)
                dve.tensor_tensor(Sf.rearrange("p (h t) -> p h t", h=4),
                                  psS[:, :].rearrange("p (h t) -> p h t", h=4),
                                  mask[:, :].rearrange("p (o t) -> p o t", o=1).to_broadcast([P, 4, P]),
                                  ALU.mult).then_inc(dve_sf, 1)

            def turned_keys(b, U, s):
                need(dve, act_kvh, b, T_KV, U, 4, 2 * (s // 4) + 2)
                dve.tensor_tensor(KTl[:, :, :].rearrange("p c d -> p (c d)"), psT[:, :],
                                  KTh[:, :, :].rearrange("p c d -> p (c d)").bitcast(F32),
                                  ALU.subtract).then_inc(dve_kvl, 1)

            def slot_a(b, U, s, n):
                m = s - 1
                it = item_of(m)
                mu, ms = m // SPU, m % SPU
                q_item = exists(n, -4, 27)
                k_item = m % 4 == 2 and exists(n, -1, 27)
                pstep = ((m + 1) // 4 + 1) % 2
                todo = jobs(b, 0, n)
                variances(todo)
                if n == -4:
                    dve.wait_ge(tab_ld, b * 32 + 32)
                if q_item:
                    need(dve, act_rot, b, T_ITEM, U, 10, it + 1)
                    dve.tensor_tensor(xq, q_tile(n and n - 1)[:, :], cosb[:, pstep, :],
                                      ALU.mult).then_inc(dve_t1, 1)
                    dve.tensor_tensor(rot, rot, sinb[:, pstep, :], ALU.mult).then_inc(dve_t2, 1)
                if k_item:
                    kstep = ((s + 1) // 4) % 2
                    need(dve, act_rot, b, T_ITEM, U, 10, it + 2)
                    dve.tensor_tensor(xk, psK[:, :], cosb[:, kstep, :], ALU.mult).then_inc(dve_t1, 1)
                    dve.tensor_tensor(vT, vT, sinb[:, kstep, :], ALU.mult).then_inc(dve_t2, 1)
                if q_item:
                    need(dve, dve_t2, b, T_ITEM, U, 10, it + 1)
                    dve.tensor_tensor(xq, xq, rot, ALU.add).then_inc(dve_x, 1)
                if k_item:
                    need(dve, dve_t2, b, T_ITEM, U, 10, it + 2)
                    dve.tensor_tensor(xk, xk, vT, ALU.add).then_inc(dve_x, 1)
                if exists(n, 0, 28):
                    mask_scores(b, U, s, n)
                if exists(n, 1, 32) and ms < SPU - 1:
                    need(dve, act_sth, b, T_STATE, U, 7, 7 * mu + ms + 1)
                    dve.tensor_tensor(Stl[:, 0, :], psSt[:, 0:P], Sth[:, 0, :].bitcast(F32), ALU.subtract)
                    dve.tensor_tensor(Stl[:, 1, :], psSt[:, P:P + 1].to_broadcast([P, P]),
                                      Sth[:, 1, :].bitcast(F32), ALU.subtract).then_inc(dve_stl, 1)
                if s % 4 == 0 and exists(n, 0, 28):
                    need(dve, act_kvh, b, T_KV, U, 4, 2 * (s // 4) + 1)
                    dve.tensor_tensor(Vl[:, :, :], psT[:, :].rearrange("p (c d) -> p c d", c=4),
                                      Vh[:, :, 0:P].bitcast(F32), ALU.subtract).then_inc(dve_kvl, 1)
                if exists(n, 1, 32):
                    need(dve, act_r0, b, T_SLOT, U, SPU, s)
                    dve.scalar_tensor_tensor(Tn, psD[:, :], EPS_DEN, r0, ALU.add, ALU.mult).then_inc(dve_T, 1)
                if q_item:
                    need(dve, act_exp, b, T_ITEM, U, 10, it + 1)
                    dve.tensor_scalar(Eq, Eq, 1.0, None, ALU.min).then_inc(dve_m, 1)
                if exists(n, 1, 32):
                    need(dve, dve_T, b, T_SLOT, U, SPU, s)
                    dve.scalar_tensor_tensor(Tn, Tn, 2.0, r0, ALU.subtract, ALU.mult).then_inc(dve_U, 1)
                if q_item:
                    need(dve, dve_m, b, T_ITEM, U, 10, it + 1)
                    need(dve, pool_fl, b, T_ITEM, U, 10, it)
                    dve.scalar_tensor_tensor(fq, xq, 0.0, Eq, ALU.max, ALU.add).then_inc(dve_f, 1)
                if k_item:
                    need(dve, act_exp, b, T_ITEM, U, 10, it + 2)
                    dve.tensor_scalar(Ek, Ek, 1.0, None, ALU.min).then_inc(dve_m, 1)
                if exists(n, 1, 32):
                    need(dve, dve_U, b, T_SLOT, U, SPU, s)
                    need(dve, pool_al, b, T_SLOT, U, SPU, m)
                    dve.scalar_tensor_tensor(of, Tn, -1.0, psO[:, :], ALU.mult, ALU.mult).then_inc(dve_a, 1)
                middle(todo)
                if k_item:
                    need(dve, dve_m, b, T_ITEM, U, 10, it + 2)
                    dve.scalar_tensor_tensor(kf, xk, 0.0, Ek, ALU.max, ALU.add).then_inc(dve_f, 1)
                if n == 28:
                    turned_keys(b, U, s)
                for job in jobs_before(b, 0, n):
                    split_x(*job)
                late(todo)
                if s == 2 and exists(n, 2, 25):
                    wlo_a(b, U, 4, Wl[:, 0, :], Wh[:, 0, :])
                if n is not None and 28 <= n <= 30:
                    mask_scores(b, U, s + 1, n + 1)
                if n == 2:
                    dve.wait_ge(y_ok, b * (T_SLOT + 1) + 1)
                if exists(n, 2, 33):
                    need(dve, pe_y, b, T_SLOT, U, SPU, s - 1)
                    t = (s - 2) % SPU
                    dve.tensor_tensor(Y[:, t, :], psY[:, :], Y[:, t, :], ALU.add).then_inc(y_ok, 1)
                if s == 9 and exists(n, 2, 25):
                    for h in range(2):
                        wlo_a(b, U + 1, h, Ol[:, h, :], Oh[:, h, :])
                if n == 1:
                    for h in range(2):
                        wlo_a(b, 0, h, Ol[:, h, :], Oh[:, h, :])
                if s % 4 == 0 and exists(n, 0, 27):
                    turned_keys(b, U, s)

            def add_down(b, U, s, n):
                if n == 5:
                    dve.wait_ge(yf_ok, b * (T_SLOT + 2) + 2)
                if exists(n, 5, 36):
                    y = s - 5
                    need(dve, pe_d, b, T_SLOT, U, SPU, y + 1)
                    t = y % TT
                    dve.tensor_tensor(YF[:, t, :], psYF[y % 2][:, :], YF[:, t, :], ALU.add).then_inc(yf_ok, 1)

            def slot_f(b, U, s, n):
                if exists(n, 1, 32):
                    i = (s - 1) % 4
                    need(dve, pe_u, b, T_SLOT, U, SPU, s)
                    need(dve, act_sg, b, T_SLOT, U, SPU, s)
                    if s >= 5:
                        d = (s - 1) // 4 - 1
                        if i < 2:
                            need(dve, pool_hl, b, 4 * NU, U, 4, 2 * d + i + 1)
                        else:
                            need(dve, dve_hl, b, 4 * NU, U, 4, 2 * d + i - 1)
                    dve.tensor_tensor(hid[:, i, :], psU[(s - 1) % 2][:, :], sg, ALU.mult).then_inc(dve_h, 1)
                todo = jobs(b, 1, n)
                if n is not None and n >= 33:
                    add_down(b, U, s, n)
                if n == 32:
                    for job in jobs_before(b, 1, n):
                        split_x(*job)
                variances(todo)

                def pair(i, c, steps):
                    need(dve, act_ab, b, T_SLOT, U, SPU, steps)
                    dve.tensor_tensor(c, ab[:, 2 * i, :], ab[:, 2 * i + 1, :], ALU.is_ge)
                    dve.tensor_tensor(Wmax[i], ab[:, 2 * i, :], ab[:, 2 * i + 1, :], ALU.max)
                    return dve.tensor_tensor(ab[:, 2 * i, :], ab[:, 2 * i, :], ab[:, 2 * i + 1, :], ALU.min)

                if s % 4 == 3 and exists(n, 3, 31):
                    pair(0, c01, s - 1).then_inc(dve_self, 1)
                if s % 4 == 0 and exists(n, 4, 32):
                    d = s // 4 - 1
                    pair(1, c23, s).then_inc(dve_self, 1)
                    k0, per = d * SELF_F, 2 * SELF_F

                    def own(k):
                        need(dve, dve_self, b, SELF, U, per, k0 + k)

                    own(2)
                    dve.tensor_tensor(pw, ab[:, 0, :], Wmax[1], ALU.is_ge).then_inc(dve_self, 1)
                    dve.tensor_tensor(qw, ab[:, 2, :], Wmax[0], ALU.is_gt).then_inc(dve_rank, 1)
                    own(3)
                    need(dve, dve_rank, b, T_STEP, U, 2, d + 1)
                    dve.tensor_tensor(rr, qw, pw, ALU.subtract).then_inc(dve_self, 1)
                    dve.tensor_tensor(pw, pw, qw, ALU.subtract).then_inc(dve_self, 1)
                    own(5)
                    dve.tensor_tensor(m0, c01, rr, ALU.is_gt).then_inc(dve_self, 1)
                    dve.tensor_tensor(m2, c23, pw, ALU.is_gt).then_inc(dve_self, 1)
                    dve.tensor_scalar(rr, rr, -1.0, 1.0, ALU.mult, ALU.add).then_inc(dve_self, 1)
                    dve.tensor_scalar(pw, pw, -1.0, 1.0, ALU.mult, ALU.add).then_inc(dve_self, 1)
                    own(6)
                    dve.tensor_tensor(hid[:, 0, :], hid[:, 0, :], m0, ALU.mult).then_inc(dve_hs, 1)
                    own(8)
                    dve.tensor_tensor(c01, c01, rr, ALU.is_lt).then_inc(dve_self, 1)
                    own(9)
                    dve.tensor_tensor(c23, c23, pw, ALU.is_lt).then_inc(dve_self, 1)
                    own(10)
                    dve.tensor_tensor(hid[:, 1, :], hid[:, 1, :], c01, ALU.mult).then_inc(dve_hs, 1)
                    own(7)
                    dve.tensor_tensor(hid[:, 2, :], hid[:, 2, :], m2, ALU.mult).then_inc(dve_hs, 1)
                    own(11)
                    dve.tensor_tensor(hid[:, 3, :], hid[:, 3, :], c23, ALU.mult).then_inc(dve_hs, 1)
                    for i in range(2, 4):
                        need(dve, act_hh, b, 8 * NU, U, 8, 4 * d + i + 1)
                        dve.tensor_tensor(big_l[:, d % 2, i, :], hid[:, i, :], big_h[:, d % 2, i, :].bitcast(F32),
                                          ALU.subtract).then_inc(dve_hl, 1)
                middle(todo)
                if n != 32:
                    for job in jobs_before(b, 1, n):
                        split_x(*job)
                late(todo)
                if n is None or n <= 32:
                    add_down(b, U, s, n)

            SELF_F = 11
            SELF = SELF_F * T_STEP

            dve.memset(eps_den[:, :], EPS_DEN)
            dve.memset(mhalf[:, :], -0.5)
            dve.memset(eps_ln[:, :], EPS_LN)
            dve.memset(rot, 1.0).then_inc(dve_const, 1)
            dve.memset(xq, 0.0).then_inc(dve_const, 1)
            dve.wait_ge(dve_const, 2)
            dve.tensor_copy(ones[:, :], rot[:, 0:P])
            dve.tensor_copy(Vh[:, :, P:P + 1], rot[:, 0:4].rearrange("p (c o) -> p c o", o=1))
            dve.tensor_copy(Vh[:, :, P + 1:P + 2],
                            xq[:, 0:4].rearrange("p (c o) -> p c o", o=1)).then_inc(const_ok, 1)
            first = [("in", 0, t) for t in range(4)]
            variances(first[0:2])
            late(first[0:2])
            variances(first[2:4])
            for t in range(4):
                split_x("in", 0, t)
                if t < 2:
                    late(first[t + 2:t + 3])
            for b in range(B):
                walk_a(dve, b, slot_a)
                walk_f(dve, b, slot_f)
            todo = jobs(B, 0, -5)
            variances(todo)
            middle(todo)

        @block.gpsimd
        def _(pool):
            eps_done = []

            def lo(dst, full, hi):
                return pool.tensor_tensor(dst, full, hi.bitcast(F32), ALU.subtract)

            def deviations(todo, second=False):
                for kind, b, t in todo:
                    k = (b * TT + t) * (2 if kind == "mid" else 1) + second
                    r = rstd[kind][:, t % 2:t % 2 + 1]
                    pool.wait_ge(dve_var[kind], k + 1)
                    pool.tensor_tensor(r, mv[kind][:, t % 2, 1:2], eps_ln[:, :], ALU.add).then_inc(pool_eps, 1)
                    eps_done.append(1)
                    pool.wait_ge(pool_eps, len(eps_done))
                    pool.tensor_tensor(r, r, mhalf[:, :], ALU.pow).then_inc(pool_rs[kind], 1)

            def add_out(todo):
                for kind, b, t in todo:
                    if kind == "out":
                        pool.wait_ge(dve_norm[kind], b * TT + t + 1)
                        pool.tensor_tensor(Y[:, t, :], YF[:, t, :], Y[:, t, :], ALU.add).then_inc(pool_out, 1)

            def wlo_a(b, U, i, dst, hi):
                need(pool, act_w, b, T_WACT_A, U, A_UNIT, i + 1)
                lo(dst, stage[:, i % RING_A, :], hi).then_inc(pool_w, 1)

            def wlo_f(b, U, i, dst, hi):
                need(pool, act_wf, b, T_W_F, U, F_UNIT, i + 1)
                lo(dst, stage[:, i % RING_F, :], hi).then_inc(pool_wf, 1)

            def split_scores(b, U, s):
                need(pool, act_sh, b, T_SLOT, U, SPU, s + 1)
                lo(Sl[s % 2], Sf, Sh[s % 2]).then_inc(pool_sl, 1)

            def slot_a(b, U, s, n):
                m = s - 1
                it = item_of(m)
                for i in first_a_pieces(b, 0, n):
                    wlo_a(b, 0, i, Wl[:, i, :], Wh[:, i, :])
                if n is not None and 29 <= n <= 31:
                    split_scores(b, U, s)
                deviations(jobs(b, 0, n))
                if n == -1:
                    if b > 0:
                        pool.wait_ge(st_out, b * TT * 16)
                    pool.memset(Y[:, :, :], 0.0).then_inc(y_ok, 1)
                if exists(n, 0, 28):
                    split_scores(b, U, s)
                if exists(n, -4, 27):
                    par, h = ((m + 1) // 4 + 1) % 2, (m + 1) % 4
                    need(pool, act_fh, b, T_ITEM, U, 10, it + 1)
                    lo(big_l[:, par, h, :], fq, big_h[:, par, h, :]).then_inc(pool_fl, 1)
                if m % 4 == 2 and exists(n, -1, 27):
                    need(pool, act_fh, b, T_ITEM, U, 10, it + 2)
                    lo(Kl[:, :], kf, Kh[:, :]).then_inc(pool_fl, 1)
                if exists(n, 1, 32):
                    need(pool, act_ah, b, T_SLOT, U, SPU, s)
                    lo(Al[:, :, :].rearrange("p h t -> p (h t)"), of,
                       Ah[:, :, :].rearrange("p h t -> p (h t)")).then_inc(pool_al, 1)
                deviations([job for job in jobs(b, 0, n) if job[0] == "mid"], second=True)
                add_out(jobs(b, 0, n))
                if s == 3 and exists(n, 2, 25):
                    wlo_a(b, U, A_PRO + 5, Wl[:, 1, :], Wh[:, 1, :])
                    wlo_a(b, U, A_PRO + 6, Wl[:, 2, :], Wh[:, 2, :])
                if s == 4 and exists(n, 2, 25):
                    wlo_a(b, U, A_PRO + 7, Wl[:, 3, :], Wh[:, 3, :])
                    wlo_a(b, U, A_PRO + 8, Wl[:, 4, :], Wh[:, 4, :])
                if s == 5 and exists(n, 2, 25):
                    wlo_a(b, U, A_PRO + 9, Wl[:, 5, :], Wh[:, 5, :])
                if s == 9 and exists(n, 2, 25):
                    for h in range(2, 4):
                        wlo_a(b, U + 1, A_PRO + h, Ol[:, h, :], Oh[:, h, :])
                if n == 1:
                    for h in range(2, 4):
                        wlo_a(b, 0, A_PRO + h, Ol[:, h, :], Oh[:, h, :])
                for i in first_f(0, n):
                    wlo_f(b, 0, i, Wl[:, w_of_piece_f[i], :], Wh[:, w_of_piece_f[i], :])

            def slot_f(b, U, s, n):
                for i in first_a_pieces(b + 1, 1, n):
                    wlo_a(b + 1, 0, i, Wl[:, i, :], Wh[:, i, :])
                if s % 4 == 0 and exists(n, 4, 32):
                    d = s // 4 - 1
                    for i in range(2):
                        need(pool, act_hh, b, 8 * NU, U, 8, 4 * d + i + 1)
                        lo(big_l[:, d % 2, i, :], hid[:, i, :], big_h[:, d % 2, i, :]).then_inc(pool_hl, 1)
                if s == 5 and exists(n, 5, 29):
                    for i in range(4):
                        wlo_f(b, U, F_PRO + i, Ol[:, i, :], Oh[:, i, :])
                deviations(jobs(b, 1, n))
                deviations([job for job in jobs(b, 1, n) if job[0] == "mid"], second=True)
                add_out(jobs(b, 1, n))
                for i in first_f(1, n):
                    wlo_f(b, 0, i, Wl[:, w_of_piece_f[i], :], Wh[:, w_of_piece_f[i], :])
                if n == 4:
                    pool.wait_ge(pe_xt, turned("mid", b, TT))
                    pool.memset(YF, 0.0).then_inc(yf_ok, 2)
                if 5 <= s <= 8 and exists(n, 5, 28):
                    i = s - 5
                    wlo_f(b, U, F_PRO + 4 + 2 * i, Wl[:, i, :], Wh[:, i, :])
                    wlo_f(b, U, F_PRO + 5 + 2 * i, Wl[:, 4 + i, :], Wh[:, 4 + i, :])

            pool.wait_ge(const_ok, 1)
            first = [("in", 0, t) for t in range(4)]
            deviations(first[0:2])
            wlo_a(0, 0, 0, Wl[:, 0, :], Wh[:, 0, :])
            deviations(first[2:4])
            for b in range(B):
                walk_a(pool, b, slot_a)
                walk_f(pool, b, slot_f)
            deviations(jobs(B, 0, -5))
            add_out(jobs(B, 0, -5))


_OUT = ((B, S, DM), "float32")


def kernel(L0_attn_x, L0_attn_Wq, L0_attn_Wk, L0_attn_Wv, L0_attn_Wo,
           L0_ffn_w_gate, L0_ffn_w_up, L0_ffn_w_down):
    import concourse.bacc as bacc
    from concourse.bass_utils import run_bass_kernel_spmd

    def f(a):
        return np.ascontiguousarray(a)

    Wq = np.asarray(L0_attn_Wq).reshape(KVH, REP, P, KT, P).transpose(0, 1, 4, 3, 2)
    Wk = np.asarray(L0_attn_Wk).reshape(KVH, P, KT, P).transpose(0, 3, 2, 1)
    Wv = np.asarray(L0_attn_Wv).reshape(KVH, P, KT, P).transpose(0, 3, 2, 1)
    Wo = np.asarray(L0_attn_Wo).reshape(DM, KVH, REP, P).transpose(1, 2, 3, 0)
    Wg = np.asarray(L0_ffn_w_gate).reshape(KT, P, NU, P, 4).transpose(2, 4, 1, 0, 3)
    Wu = np.asarray(L0_ffn_w_up).reshape(KT, P, NU, P, 4).transpose(2, 4, 1, 0, 3)
    Wd = np.asarray(L0_ffn_w_down).reshape(NU, P, 4, DM).transpose(0, 2, 1, 3)
    power = np.arange(0, P, 2, dtype=np.float32) / np.float32(P)
    freq = np.float32(1) / np.power(10000.0, power.astype(np.float64)).astype(np.float32)
    angle = np.outer(freq, np.arange(S, dtype=np.float32)).astype(np.float64)
    cos = np.cos(angle).astype(np.float32)
    sin = np.sin(angle).astype(np.float32)
    place = np.arange(P)
    arrays = {
        "x": f(L0_attn_x),
        "wq": f(Wq).reshape(NU, 4, P, W), "wk": f(Wk).reshape(NU, P, W), "wv": f(Wv).reshape(NU, P, W),
        "wo": f(Wo), "wg": f(Wg).reshape(NU, 4, P, W), "wu": f(Wu).reshape(NU, 4, P, W), "wd": f(Wd),
        "cos_t": np.concatenate([cos, cos]), "sin_t": np.concatenate([-sin, sin]),
        "causal": (place[:, None] <= place[None, :]).astype(np.float32),
        "eye": np.eye(P, dtype=np.float32),
    }
    nc = bacc.Bacc("TRN2", target_bir_lowering=False, num_devices=1)
    args = [nc.dram_tensor(n, a.shape, mybir.dt.from_np(a.dtype), kind="ExternalInput").ap()
            for n, a in arrays.items()]
    shape, dtype = _OUT
    args.append(nc.dram_tensor("out", shape, mybir.dt.from_np(np.dtype(dtype)), kind="ExternalOutput").ap())
    build(nc, *args)
    r = run_bass_kernel_spmd(nc, [arrays], core_ids=[0])
    return r.results[0]["out"]
```
